# Optimizing a Trainium2 kernel written in Bass

```python
import numpy as np
import jax
import jax.numpy as jnp

def _softmax(x, axis=-1):
    return jax.nn.softmax(x, axis=axis)

def _gelu(x):
    return jax.nn.gelu(x, approximate=True)

def _silu(x):
    return jax.nn.silu(x)

def _sigmoid(x):
    return jax.nn.sigmoid(x)

def _layernorm(x, axis=-1, eps=1e-05):
    m = jnp.mean(x, axis=axis, keepdims=True)
    v = jnp.var(x, axis=axis, keepdims=True)
    return (x - m) / jnp.sqrt(v + eps)

def _scatter_add(tgt, idx, src, axis=0):
    return tgt.at[idx].add(src)

def _segment_sum(src, seg, n):
    return jax.ops.segment_sum(src, seg, n)
kernel_name = 'mk_macaron_d2_jaxref_r8_9ea596'

def setup_inputs(seed: int=0):
    np.random.seed(seed)
    _w = jnp.asarray

    def _L0_attn_setup():
        import jax, jax.numpy as jnp
        import numpy as np
        N_HEAD = 16
        HEAD_SIZE = 128
        EMBED = 128
        MULTI_HEAD_SIZE = HEAD_SIZE // N_HEAD
        B, S = (4, 256)
        key = jax.random.key(seed)
        k1, k2, k3, k4 = jax.random.split(key, 4)
        x = jax.random.normal(k1, (B, S, EMBED), dtype=jnp.float32)
        w_qkv = jax.random.normal(k2, (3 * HEAD_SIZE, EMBED), dtype=jnp.float32) * 0.02
        w_proj = jax.random.normal(k3, (EMBED, HEAD_SIZE), dtype=jnp.float32) * 0.02
        b_proj = jax.random.normal(k4, (EMBED,), dtype=jnp.float32) * 0.02
        return {'x': x, 'w_qkv': w_qkv, 'w_proj': w_proj, 'b_proj': b_proj}
    _L0_attn_in = _L0_attn_setup()

    def _L0_ffn_setup():
        import jax, jax.numpy as jnp
        import numpy as np
        DIM = 128

        def _reference_tuple_inner(x, W_r, W_k, W_v, mu_r, mu_k):
            B, T, C = x.shape
            x_prev = jnp.concatenate([jnp.zeros((B, 1, C), x.dtype), x[:, :-1, :]], axis=1)
            xr = mu_r * x + (1.0 - mu_r) * x_prev
            xk = mu_k * x + (1.0 - mu_k) * x_prev
            r = jax.nn.sigmoid(jnp.einsum('btc,dc->btd', xr, W_r))
            k = jnp.einsum('btc,dc->btd', xk, W_k)
            k_act = jnp.square(jax.nn.relu(k))
            out = r * jnp.einsum('btc,dc->btd', k_act, W_v)
            new_state = x[:, -1, :]
            return (out, new_state)
        key = jax.random.key(seed)
        ks = jax.random.split(key, 6)
        B, T, C = (8, 256, DIM)
        x = jax.random.normal(ks[0], (B, T, C), dtype=jnp.float32)
        s = 1.0 / np.sqrt(C)
        W_r = jax.random.uniform(ks[1], (C, C), jnp.float32, -s, s)
        W_k = jax.random.uniform(ks[2], (C, C), jnp.float32, -s, s)
        W_v = jax.random.uniform(ks[3], (C, C), jnp.float32, -s, s)
        mu_r = jax.random.uniform(ks[4], (C,), jnp.float32)
        mu_k = jax.random.uniform(ks[5], (C,), jnp.float32)
        return {'x': x, 'W_r': W_r, 'W_k': W_k, 'W_v': W_v, 'mu_r': mu_r, 'mu_k': mu_k}
    _L0_ffn_in = _L0_ffn_setup()

    def _L1_attn_setup():
        import jax, jax.numpy as jnp
        import numpy as np
        B, S, DM = (2, 256, 128)
        H, D = (16, 64)

        def _rel_pos_enc(seq_len: int, dim: int) -> jnp.ndarray:
            positions = jnp.arange(seq_len, dtype=jnp.float32)[:, None]
            div_term = jnp.exp(jnp.arange(0, dim, 2, dtype=jnp.float32) * -(np.log(10000.0) / dim))
            pe = jnp.zeros((seq_len, dim), dtype=jnp.float32)
            pe = pe.at[:, 0::2].set(jnp.sin(positions * div_term))
            pe = pe.at[:, 1::2].set(jnp.cos(positions * div_term))
            return pe
        key = jax.random.key(seed)
        k1, k2, k3 = jax.random.split(key, 3)
        x = jax.random.normal(k1, (B, S, DM), dtype=jnp.float32)
        W_qkv = jax.random.normal(k2, (DM, 3 * H * D), dtype=jnp.float32) / np.sqrt(DM)
        b_qkv = jnp.zeros((3 * H * D,), dtype=jnp.float32)
        W_out = jax.random.normal(k3, (H * D, DM), dtype=jnp.float32) / np.sqrt(H * D)
        b_out = jnp.zeros((DM,), dtype=jnp.float32)
        return {'x': x, 'W_qkv': W_qkv, 'b_qkv': b_qkv, 'W_out': W_out, 'b_out': b_out}
    _L1_attn_in = _L1_attn_setup()

    def _L1_ffn_setup():
        import jax, jax.numpy as jnp
        import numpy as np
        THRESH_FACTOR = 0.7

        def ternary_quantize(w):
            delta = THRESH_FACTOR * jnp.mean(jnp.abs(w))
            return jnp.where(w > delta, 1.0, jnp.where(w < -delta, -1.0, 0.0)).astype(w.dtype)
        key = jax.random.key(seed)
        k1, k2, k3 = jax.random.split(key, 3)
        B, S, D_IN, D_OUT = (8, 512, 128, 128)
        inp = {'input': jax.random.normal(k1, (B, S, D_IN), dtype=jnp.float32), 'weight': jax.random.normal(k2, (D_OUT, D_IN), dtype=jnp.float32) * (1.0 / np.sqrt(D_IN)), 'alpha': jnp.ones((1,), dtype=jnp.float32), 'bias': jax.random.normal(k3, (D_OUT,), dtype=jnp.float32) * (1.0 / np.sqrt(D_IN))}
        return inp
    _L1_ffn_in = _L1_ffn_setup()
    _d = {'L0_attn_x': _L0_attn_in['x'], 'L0_attn_w_qkv': _L0_attn_in['w_qkv'], 'L0_attn_w_proj': _L0_attn_in['w_proj'], 'L0_attn_b_proj': _L0_attn_in['b_proj'], 'L0_ffn_W_r': _L0_ffn_in['W_r'], 'L0_ffn_W_k': _L0_ffn_in['W_k'], 'L0_ffn_W_v': _L0_ffn_in['W_v'], 'L0_ffn_mu_r': _L0_ffn_in['mu_r'], 'L0_ffn_mu_k': _L0_ffn_in['mu_k'], 'L1_attn_W_qkv': _L1_attn_in['W_qkv'], 'L1_attn_b_qkv': _L1_attn_in['b_qkv'], 'L1_attn_W_out': _L1_attn_in['W_out'], 'L1_attn_b_out': _L1_attn_in['b_out'], 'L1_ffn_weight': _L1_ffn_in['weight'], 'L1_ffn_alpha': _L1_ffn_in['alpha'], 'L1_ffn_bias': _L1_ffn_in['bias']}
    _x0 = _d['L0_attn_x']
    _d['L0_attn_x'] = jax.random.normal(jax.random.fold_in(jax.random.key(seed), 1), (32, 256, 128), dtype=_x0.dtype)
    del _x0
    return _d

def reference(L0_attn_x, L0_attn_w_qkv, L0_attn_w_proj, L0_attn_b_proj, L0_ffn_W_r, L0_ffn_W_k, L0_ffn_W_v, L0_ffn_mu_r, L0_ffn_mu_k, L1_attn_W_qkv, L1_attn_b_qkv, L1_attn_W_out, L1_attn_b_out, L1_ffn_weight, L1_ffn_alpha, L1_ffn_bias):

    def _L0_attn_ref(x, w_qkv, w_proj, b_proj):
        import jax, jax.numpy as jnp
        import numpy as np
        N_HEAD = 16
        HEAD_SIZE = 128
        EMBED = 128
        MULTI_HEAD_SIZE = HEAD_SIZE // N_HEAD
        B, S = (4, 256)
        qkv = jnp.einsum('bse,he->bsh', x, w_qkv)
        q, k, v = jnp.split(qkv, 3, axis=-1)
        scale = 1.0 / np.sqrt(MULTI_HEAD_SIZE).astype(np.float32)
        scores = jnp.einsum('bqh,bkh->bqk', q, k) * scale
        probs = jax.nn.softmax(scores, axis=-1)
        out = jnp.einsum('bqk,bkh->bqh', probs, v)
        Bn, Sn, H = out.shape
        out = jnp.swapaxes(out, 1, 2).reshape(Bn, Sn, H)
        out = jnp.einsum('bsh,eh->bse', out, w_proj) + b_proj
        return out

    def _L0_ffn_ref(x, W_r, W_k, W_v, mu_r, mu_k):
        import jax, jax.numpy as jnp
        import numpy as np
        DIM = 128

        def _reference_tuple_inner(x, W_r, W_k, W_v, mu_r, mu_k):
            B, T, C = x.shape
            x_prev = jnp.concatenate([jnp.zeros((B, 1, C), x.dtype), x[:, :-1, :]], axis=1)
            xr = mu_r * x + (1.0 - mu_r) * x_prev
            xk = mu_k * x + (1.0 - mu_k) * x_prev
            r = jax.nn.sigmoid(jnp.einsum('btc,dc->btd', xr, W_r))
            k = jnp.einsum('btc,dc->btd', xk, W_k)
            k_act = jnp.square(jax.nn.relu(k))
            out = r * jnp.einsum('btc,dc->btd', k_act, W_v)
            new_state = x[:, -1, :]
            return (out, new_state)
        return _reference_tuple_inner(x, W_r, W_k, W_v, mu_r, mu_k)[0]

    def _L1_attn_ref(x, W_qkv, b_qkv, W_out, b_out):
        import jax, jax.numpy as jnp
        import numpy as np
        B, S, DM = (2, 256, 128)
        H, D = (16, 64)

        def _rel_pos_enc(seq_len: int, dim: int) -> jnp.ndarray:
            positions = jnp.arange(seq_len, dtype=jnp.float32)[:, None]
            div_term = jnp.exp(jnp.arange(0, dim, 2, dtype=jnp.float32) * -(np.log(10000.0) / dim))
            pe = jnp.zeros((seq_len, dim), dtype=jnp.float32)
            pe = pe.at[:, 0::2].set(jnp.sin(positions * div_term))
            pe = pe.at[:, 1::2].set(jnp.cos(positions * div_term))
            return pe
        b, s, _ = x.shape
        qkv = x @ W_qkv + b_qkv
        qkv = qkv.reshape(b, s, 3, H, D)
        q, k, v = (qkv[:, :, 0], qkv[:, :, 1], qkv[:, :, 2])
        pos_enc = _rel_pos_enc(s, D)
        k = k + pos_enc[None, :, None, :]
        scale = jnp.sqrt(jnp.asarray(D, dtype=x.dtype))
        scores = jnp.einsum('bqhd,bkhd->bhqk', q, k) / scale
        attn = jax.nn.softmax(scores, axis=-1)
        out = jnp.einsum('bhqk,bkhd->bqhd', attn, v)
        out = out.reshape(b, s, H * D)
        return out @ W_out + b_out

    def _L1_ffn_ref(input, weight, alpha, bias):
        import jax, jax.numpy as jnp
        import numpy as np
        THRESH_FACTOR = 0.7

        def ternary_quantize(w):
            delta = THRESH_FACTOR * jnp.mean(jnp.abs(w))
            return jnp.where(w > delta, 1.0, jnp.where(w < -delta, -1.0, 0.0)).astype(w.dtype)
        w_ternary = ternary_quantize(weight)
        w_eff = w_ternary * alpha
        out = jnp.einsum('bsd,od->bso', input, w_eff) + bias
        return out
    x = L0_attn_x
    x = x + 0.5 * _L0_ffn_ref(_layernorm(x, axis=-1), L0_ffn_W_r, L0_ffn_W_k, L0_ffn_W_v, L0_ffn_mu_r, L0_ffn_mu_k)
    x = x + _L0_attn_ref(_layernorm(x, axis=-1), L0_attn_w_qkv, L0_attn_w_proj, L0_attn_b_proj)
    x = x + 0.5 * _L0_ffn_ref(_layernorm(x, axis=-1), L0_ffn_W_r, L0_ffn_W_k, L0_ffn_W_v, L0_ffn_mu_r, L0_ffn_mu_k)
    x = x + 0.5 * _L1_ffn_ref(_layernorm(x, axis=-1), L1_ffn_weight, L1_ffn_alpha, L1_ffn_bias)
    x = x + _L1_attn_ref(_layernorm(x, axis=-1), L1_attn_W_qkv, L1_attn_b_qkv, L1_attn_W_out, L1_attn_b_out)
    x = x + 0.5 * _L1_ffn_ref(_layernorm(x, axis=-1), L1_ffn_weight, L1_ffn_alpha, L1_ffn_bias)
    return x

_drawn_inputs = setup_inputs


def setup_inputs(seed=0):
    import zlib

    import numpy as np

    out = dict(_drawn_inputs(seed))
    spreads = {'L1_attn_b_qkv': (0.0, 0.39), 'L1_attn_b_out': (0.0, 0.389)}
    factors = {'L0_attn_w_qkv': 8.0,
     'L0_attn_w_proj': 8.0,
     'L0_attn_b_proj': 9.632,
     'L0_ffn_W_r': 3.163,
     'L0_ffn_mu_r': 6.209,
     'L1_ffn_bias': 4.104}
    for name, (base, spread) in spreads.items():
        noise = np.random.default_rng([zlib.crc32(name.encode()), seed]).standard_normal(out[name].shape)
        drawn = base * np.exp(spread * noise) if base else spread * noise
        out[name] = jnp.asarray(drawn.astype(out[name].dtype))
    for name, factor in factors.items():
        out[name] = (out[name] * factor).astype(out[name].dtype)
    return out
```

```python
from contextlib import ExitStack

import numpy as np

import concourse.bass as bass
from concourse import mybir

F32 = mybir.dt.float32
F32R = mybir.dt.float32r
ALU = mybir.AluOpType
ACT = mybir.ActivationFunctionType
AX_X = mybir.AxisListType.X

P = 128
NB, S, C = 32, 256, 128
J = S // P
H, D = 16, 64
PAIRS = H // 2
G = 2
HG = H // G
PG = PAIRS // G
VW = 96
ATTN0_SCALE = float(1.0 / np.sqrt(8.0).astype(np.float32))
EPS = 1e-5
LOAD = 4


class Step:

    def __init__(self, half, parity):
        self.half, self.parity = half, parity

    def back(self, lag):
        n = self.parity - lag
        return Step(self.half + (n - n % 2) // 2, n % 2)

    @property
    def n(self):
        return self.half * 2 + self.parity

    def within(self, count):
        return not isinstance(self.half, int) or 0 <= self.n < count


def run_steps(eng, count, lag, step):
    for t in range(lag):
        step(Step(t // 2, t % 2))
    with eng.Fori(lag // 2, count // 2) as half:
        step(Step(half, 0))
        step(Step(half, 1))
    for t in range(count, count + lag):
        step(Step(t // 2, t % 2))


def wait(eng, sem, value):
    if isinstance(value, int) and value <= 0:
        return
    eng.wait_ge(sem, value)


def macaron_kernel(nc, x_in, w_qkv0, w_proj0, b_proj0, W_r, W_k, W_v, mu_r, mu_k,
                   W_qkv1, b_qkv1, W_out1, b_out1, w_tern, alpha, bias_tern, pos_t, x_out):
    ctx = ExitStack()
    with ctx:
        def sb(name, shape, dt=F32):
            return ctx.enter_context(nc.sbuf_tensor(name, shape, dt))

        def sem(name):
            return ctx.enter_context(nc.semaphore(name))

        x = sb("x", [P, NB, J, C])
        ident = sb("ident", [P, P])
        ones = sb("ones", [P, P])
        stats = sb("stats", [P, NB * J, 6])
        rstd = sb("rstd", [P, NB * J])
        nbias = sb("nbias", [P, NB * J])
        lnt = sb("lnt", [P, 3, NB * J])

        w_raw = sb("w_raw", [P, 8, P])
        wT = sb("wT", [P, 8, P])
        WQ, WK, WV, WP, FR, FK, FV, TW = range(8)
        wr_now, wr_prev = sb("wr_now", [P, P]), sb("wr_prev", [P, P])
        wk_now, wk_prev = sb("wk_now", [P, P]), sb("wk_prev", [P, P])
        mu = sb("mu", [P, 4])
        bproj_b = sb("bproj_b", [P, J, C])
        bout_b = sb("bout_b", [P, J, C])
        btern_b = sb("btern_b", [P, J, C])
        alpha_b = sb("alpha_b", [P, 1])
        tern = sb("tern", [P, 4])
        ternm = sb("ternm", [P, P])

        xn = sb("xn", [P, 2, J, C])
        xT = sb("xT", [P, 2, 1 + S])

        banks = [ctx.enter_context(nc.psum_tensor(f"bank{i}", [P, 512], F32)) for i in range(8)]

        def halves(b, w=C):
            return banks[b][:, 0:J * w].rearrange("p (j c) -> p j c", j=J)

        block_entry = sem("consts_ready")
        loaded = [sem(f"x_loaded{i}") for i in range(NB // LOAD)]
        stored = sem("x_stored")
        w_loaded = sem("w_loaded")
        ident_zeroed = sem("ident_zeroed")
        wT_ready = sem("wT_ready")
        w_ready = sem("w_ready")
        chain = sem("dve_chain")
        ln_var = sem("ln_var")
        ln_std = sem("ln_std")
        ln_ready = sem("ln_ready")
        tern_sum = sem("tern_sum")

        xin_v = x_in.rearrange("b (p j) c -> p b (j c)", j=J)
        xout_v = x_out.rearrange("b (p j) c -> p b (j c)", j=J)
        x_flat = x[:, :, :, :].rearrange("p b j c -> p b (j c)")
        x_chunks = x[:, :, :, :].rearrange("p b j c -> p (b j) c")

        chain_count = [0]

        def chained(dve, ins):
            chain_count[0] += 1
            ins.then_inc(chain, 1)
            dve.wait_ge(chain, chain_count[0])

        def setup_sync(sp):
            for k in range(3):
                sp.dma_start(w_raw[:, WQ + k, :], w_qkv0[k * P:(k + 1) * P, :]).then_inc(w_loaded, 16)
            for k, w in ((WP, w_proj0), (FR, W_r), (FK, W_k), (FV, W_v), (TW, w_tern)):
                sp.dma_start(w_raw[:, k, :], w).then_inc(w_loaded, 16)
            sp.dma_start(mu[:, 0:1], mu_r.rearrange("(c o) -> c o", o=1)).then_inc(w_loaded, 16)
            sp.dma_start(mu[:, 1:2], mu_k.rearrange("(c o) -> c o", o=1)).then_inc(w_loaded, 16)
            for tile, b in ((bproj_b, b_proj0), (bout_b, b_out1), (btern_b, bias_tern)):
                row = b.rearrange("(o c) -> o c", o=1).to_broadcast([P, C])
                for j in range(J):
                    sp.dma_start(tile[:, j, :], row).then_inc(w_loaded, 16)
            sp.dma_start(alpha_b[:, :], alpha.rearrange("(o c) -> o c", o=1).to_broadcast([P, 1])).then_inc(w_loaded, 16)
            for b in range(0, NB, LOAD):
                sp.dma_start(x_flat[:, b:b + LOAD, :], xin_v[:, b:b + LOAD, :]).then_inc(loaded[b // LOAD], 16)

        N_WDMA = 3 + 5 + 2 + 3 * J + 1

        def setup_pool(pool):
            pool.memset(ident[:, :], 0.0).then_inc(ident_zeroed, 1)
            pool.wait_ge(ident_zeroed, 1)
            pool.affine_select(out=ident[:, :], in_=ident[:, :], compare_op=ALU.not_equal, fill=1.0, base=0,
                               pattern=[[-1, P]], channel_multiplier=1).then_inc(block_entry, 1)
            pool.memset(xT[:, :, 0:1], 0.0).then_inc(block_entry, 1)
            pool.memset(ones[:, :], 1.0).then_inc(block_entry, 1)

        def setup_pe(pe):
            pe.wait_ge(w_loaded, 16 * N_WDMA)
            pe.wait_ge(block_entry, 3)
            for k in range(8):
                mm = pe.transpose(banks[k // 4][:, (k % 4) * P:(k % 4 + 1) * P], w_raw[:, k, :], ident[:, :])
            mm.then_inc(wT_ready, 1)
            pe.wait_ge(tern_sum, 1)
            pe.matmul(banks[2][:, 0:1], ones[:, :], tern[:, 0:1], start=True, stop=True).then_inc(tern_sum, 1)

        def setup_dve(dve):
            dve.wait_ge(w_loaded, 16 * N_WDMA)
            dve.tensor_reduce(tern[:, 0:1], w_raw[:, TW, :], AX_X, ALU.add,
                              apply_absolute_value=True).then_inc(tern_sum, 1)
            dve.tensor_scalar(mu[:, 2:4], mu[:, 0:2], -1.0, 1.0, ALU.mult, ALU.add).then_inc(chain, 1)
            chain_count[0] += 1
            dve.wait_ge(wT_ready, 1)
            for half in range(2):
                dve.tensor_copy(wT[:, 4 * half:4 * half + 4, :],
                                banks[half][:, :].rearrange("p (k c) -> p k c", k=4)).then_inc(chain, 1)
                chain_count[0] += 1
            dve.wait_ge(chain, chain_count[0])
            for w, now, prev, m in ((FR, wr_now, wr_prev, 0), (FK, wk_now, wk_prev, 1)):
                dve.tensor_scalar(now[:, :], wT[:, w, :], mu[:, m:m + 1], None, ALU.mult).then_inc(w_ready, 1)
                dve.tensor_scalar(prev[:, :], wT[:, w, :], mu[:, 2 + m:3 + m], None, ALU.mult).then_inc(w_ready, 1)
            dve.tensor_scalar(wT[:, FV, :], wT[:, FV, :], 0.5, None, ALU.mult).then_inc(w_ready, 1)
            dve.tensor_scalar(btern_b[:, :, :], btern_b[:, :, :], 0.5, None, ALU.mult).then_inc(w_ready, 1)
            dve.wait_ge(tern_sum, 2)
            chained(dve, dve.tensor_scalar(tern[:, 1:2], banks[2][:, 0:1], 1.0 / (C * C), 0.7, ALU.mult, ALU.mult))
            chained(dve, dve.tensor_scalar(tern[:, 2:3], tern[:, 1:2], -1.0, None, ALU.mult))
            chained(dve, dve.tensor_scalar(ternm[:, :], wT[:, TW, :], tern[:, 2:3], None, ALU.is_lt))
            chained(dve, dve.scalar_tensor_tensor(out=wT[:, TW, :], in0=wT[:, TW, :], scalar=tern[:, 1:2],
                                                  in1=ternm[:, :], op0=ALU.is_gt, op1=ALU.subtract))
            dve.tensor_scalar(wT[:, TW, :], wT[:, TW, :], alpha_b[:, 0:1], 0.5, ALU.mult, ALU.mult).then_inc(w_ready, 1)
            for b in range(NB):
                if b % LOAD == 0:
                    dve.wait_ge(loaded[b // LOAD], 16)
                for j in range(J):
                    dve.bn_stats(stats[:, b * J + j, :], x[:, b, j, :]).then_inc(chain, 1)
                    chain_count[0] += 1

        N_WREADY = 7
        ln_done = [0]

        def layer_consts_dve(dve):
            k = ln_done[0]
            ln_done[0] += 1
            me, mo = stats[:, :, 1], stats[:, :, 4]
            m2e, m2o = stats[:, :, 2], stats[:, :, 5]
            a, b, c = lnt[:, 0, :], lnt[:, 1, :], lnt[:, 2, :]
            dve.wait_ge(chain, chain_count[0])
            chained(dve, dve.tensor_tensor(a, me, mo, ALU.subtract))
            chained(dve, dve.tensor_tensor(b, a, a, ALU.mult))
            chained(dve, dve.tensor_tensor(a, m2e, m2o, ALU.add))
            chained(dve, dve.tensor_scalar(a, a, 1.0 / C, EPS, ALU.mult, ALU.add))
            chained(dve, dve.scalar_tensor_tensor(out=c, in0=b, scalar=0.25, in1=a, op0=ALU.mult, op1=ALU.add))
            chained(dve, dve.tensor_tensor(b, me, mo, ALU.add))
            dve.tensor_copy(a, c).then_inc(ln_var, 1)
            dve.wait_ge(ln_std, k + 1)
            chained(dve, dve.reciprocal(a, rstd[:, :]))
            chained(dve, dve.tensor_tensor(nbias[:, :], a, a, ALU.mult))
            chained(dve, dve.tensor_tensor(nbias[:, :], nbias[:, :], c, ALU.mult))
            chained(dve, dve.tensor_scalar(nbias[:, :], nbias[:, :], -0.5, 1.5, ALU.mult, ALU.add))
            chained(dve, dve.tensor_tensor(rstd[:, :], a, nbias[:, :], ALU.mult))
            dve.scalar_tensor_tensor(out=nbias[:, :], in0=b, scalar=-0.5, in1=rstd[:, :],
                                     op0=ALU.mult, op1=ALU.mult).then_inc(ln_ready, 1)
            dve.wait_ge(ln_ready, k + 1)

        def layer_consts_act(act, k):
            act.wait_ge(ln_var, k + 1)
            act.activation(rstd[:, :], lnt[:, 0, :], ACT.Sqrt).then_inc(ln_std, 1)

        def normalise(eng, out, n):
            for j in range(J):
                at = n * J + j
                ins = eng.tensor_scalar(out[:, j, :], x_chunks[:, bass.ds(at, 1), :].rearrange("p o c -> p (o c)"),
                                        rstd[:, bass.ds(at, 1)], nbias[:, bass.ds(at, 1)], ALU.mult, ALU.add)
            return ins

        def add_stats(dve, n, sems):
            for j in range(J):
                at = n * J + j
                dve.bn_stats(stats[:, bass.ds(at, 1), :].rearrange("p o s -> p (o s)"),
                             x_chunks[:, bass.ds(at, 1), :].rearrange("p o c -> p (o c)")).then_inc(sems, 1)

        def seq(n):
            return x[:, bass.ds(n, 1), :, :].rearrange("p o j c -> p (o j) c")

        def ffn_layer(layer):
            xn_ready, t_ready, xT_ready = sem(f"f{layer}_xn_ready"), sem(f"f{layer}_t_ready"), sem(f"f{layer}_xT_ready")
            k_ready, r_ready = sem(f"f{layer}_k_ready"), sem(f"f{layer}_r_ready")
            relu_ready, gate_ready = sem(f"f{layer}_relu_ready"), sem(f"f{layer}_gate_ready")
            kact_ready, kv_ready = sem(f"f{layer}_kact_ready"), sem(f"f{layer}_kv_ready")
            gated, updated, done = sem(f"f{layer}_gated"), sem(f"f{layer}_updated"), sem(f"f{layer}_stats")
            LAG = 4
            T_BANK, K_BANK, R_BANK, KV_BANK = (0, 1), (2, 3), (4, 5), (6, 7)

            def pool(eng):
                pass

            def pe(eng):
                if layer == 0:
                    eng.wait_ge(w_ready, N_WREADY)

                def step(t):
                    v = t.back(2)
                    if v.within(NB):
                        s = v.parity
                        eng.wait_ge(kact_ready, v.n + 1)
                        wait(eng, gated, v.n - 1)
                        for j in range(J):
                            mm = eng.matmul(halves(KV_BANK[s])[:, j, :], kact[:, s, j::J], wT[:, FV, :],
                                            start=True, stop=True)
                        mm.then_inc(kv_ready, 1)
                    k = t.back(1)
                    if k.within(NB):
                        s = k.parity
                        eng.wait_ge(xT_ready, k.n + 1)
                        wait(eng, relu_ready, k.n - 1)
                        wait(eng, kact_ready, k.n - 1)
                        eng.matmul(banks[K_BANK[s]][:, 0:S], wk_now[:, :], xT[:, s, 1:1 + S], start=True, stop=False)
                        eng.matmul(banks[K_BANK[s]][:, 0:S], wk_prev[:, :], xT[:, s, 0:S], start=False,
                                   stop=True).then_inc(k_ready, 1)
                        wait(eng, gate_ready, k.n - 1)
                        for j in range(J):
                            eng.matmul(halves(R_BANK[s])[:, j, :], xT[:, s, 1 + j::J], wr_now[:, :],
                                       start=True, stop=False)
                            mm = eng.matmul(halves(R_BANK[s])[:, j, :], xT[:, s, j:S:J], wr_prev[:, :],
                                            start=False, stop=True)
                        mm.then_inc(r_ready, 1)
                    if t.within(NB):
                        eng.wait_ge(xn_ready, t.n + 1)
                        wait(eng, xT_ready, t.n - 1)
                        for j in range(J):
                            mm = eng.transpose(halves(T_BANK[t.parity])[:, j, :], xn[:, t.parity, j, :], ident[:, :])
                        mm.then_inc(t_ready, 1)
                run_steps(eng, NB, LAG, step)

            def act(eng):
                layer_consts_act(eng, layer)

                def step(t):
                    k = t.back(1)
                    if k.within(NB):
                        s = k.parity
                        eng.wait_ge(k_ready, k.n + 1)
                        wait(eng, kact_ready, k.n - 1)
                        eng.activation(relu[:, s, :], banks[K_BANK[s]][:, 0:S], ACT.Relu).then_inc(relu_ready, 1)
                        eng.wait_ge(r_ready, k.n + 1)
                        wait(eng, gated, k.n - 1)
                        eng.activation(gate[:, s, :, :], halves(R_BANK[s]), ACT.Sigmoid).then_inc(gate_ready, 1)
                    if t.within(NB):
                        s = t.parity
                        eng.wait_ge(t_ready, t.n + 1)
                        wait(eng, r_ready, t.n - 1)
                        eng.copy(xT[:, s, 1:1 + S].rearrange("c (p j) -> c j p", j=J),
                                 halves(T_BANK[s])).then_inc(xT_ready, 1)
                run_steps(eng, NB, LAG, step)

            def dve(eng):
                def step(t):
                    if t.within(NB):
                        wait(eng, t_ready, t.n - 1)
                        normalise(eng, xn[:, t.parity], t.n).then_inc(xn_ready, 1)
                    v = t.back(2)
                    if v.within(NB):
                        s = v.parity
                        eng.wait_ge(kv_ready, v.n + 1)
                        eng.wait_ge(gate_ready, v.n + 1)
                        wait(eng, updated, v.n - 1)
                        eng.tensor_tensor(branch[:, s, :, :], halves(KV_BANK[s]), gate[:, s, :, :],
                                          ALU.mult).then_inc(gated, 1)
                    k = t.back(1)
                    if k.within(NB):
                        s = k.parity
                        eng.wait_ge(relu_ready, k.n + 1)
                        wait(eng, kv_ready, k.n - 1)
                        eng.tensor_tensor(kact[:, s, :], relu[:, s, :], relu[:, s, :], ALU.mult).then_inc(kact_ready, 1)
                    if v.within(NB):
                        eng.wait_ge(gated, v.n + 1)
                        eng.tensor_tensor(seq(v.n), seq(v.n), branch[:, v.parity, :, :], ALU.add).then_inc(updated, 1)
                        eng.wait_ge(updated, v.n + 1)
                        add_stats(eng, v.n, done)
                run_steps(eng, NB, LAG, step)
                eng.wait_ge(done, J * NB)

            return pool, pe, act, dve

        work = sb("work", [P, 8 * 2 * S])

        def tile(at, shape):
            n = int(np.prod(shape))
            v = work[:, at * 2 * S:at * 2 * S + n]
            names = "abcd"[:len(shape)]
            sizes = {k: d for k, d in zip(names[1:], shape[1:])}
            return v.rearrange(f"p ({' '.join(names)}) -> p {' '.join(names)}", **sizes)

        relu, gate = tile(0, [2, S]), tile(1, [2, J, C])
        kact, branch = tile(2, [2, S]), tile(3, [2, J, C])

        qk = tile(0, [2, 2, S])
        vrow = tile(2, [2, J, C])
        nmax = sb("nmax", [P, 2, J])
        nmax_s = sb("nmax_s", [P, 2, J])
        den = sb("den", [P, 2, J])
        rden = sb("rden", [P, 2, J])
        prob = tile(3, [2, J, S])
        probT = tile(5, [2, J, S])
        orow = tile(7, [2, J, C])

        def attn0_layer(layer):
            names = ("xn_ready t_ready xT_ready qk_ready qk_copied v_ready v_copied s_ready max_ready bias_ready "
                     "exp_ready den_ready pT_ready pT_copied o_ready o_copied y_ready updated stats xb_ready").split()
            q = {n: sem(f"a{layer}_{n}") for n in names}
            LAG = 6
            T_BANK, QK_BANK, V_BANK, S_BANK, PT_BANK, O_BANK, Y_BANK = range(7)

            def pool(eng):
                eng.wait_ge(ln_ready, layer + 1)

                def step(t):
                    if t.within(NB):
                        eng.wait_ge(q["xn_ready"], t.n + 1)
                        eng.tensor_tensor(seq(t.n), seq(t.n), bproj_b[:, :, :], ALU.add).then_inc(q["xb_ready"], 1)
                run_steps(eng, NB, LAG, step)

            def pe(eng):
                def step(t):
                    y = t.back(4)
                    if y.within(NB):
                        eng.wait_ge(q["o_copied"], y.n + 1)
                        wait(eng, q["updated"], y.n)
                        for j in range(J):
                            mm = eng.matmul(halves(Y_BANK)[:, j, :], orow[:, y.parity, j, :], wT[:, WP, :],
                                            start=True, stop=True)
                        mm.then_inc(q["y_ready"], 1)
                    s_ = t.back(2)
                    if s_.within(NB):
                        s = s_.parity
                        eng.wait_ge(q["qk_copied"], s_.n + 1)
                        wait(eng, q["max_ready"], s_.n)
                        wait(eng, q["exp_ready"], J * s_.n)
                        for j in range(J):
                            mm = eng.matmul(halves(S_BANK, S)[:, j, :], qk[:, s, 0, j * P:(j + 1) * P], qk[:, s, 1, :],
                                            start=True, stop=True)
                        mm.then_inc(q["s_ready"], 1)
                    o = t.back(3)
                    if o.within(NB):
                        s = o.parity
                        eng.wait_ge(q["exp_ready"], J * (o.n + 1))
                        wait(eng, q["pT_copied"], o.n)
                        for c in range(J):
                            for j in range(J):
                                mm = eng.transpose(halves(PT_BANK, S)[:, c, j * P:(j + 1) * P],
                                                   prob[:, s, j, c * P:(c + 1) * P], ident[:, :])
                        mm.then_inc(q["pT_ready"], 1)
                    k = t.back(1)
                    if k.within(NB):
                        s = k.parity
                        eng.wait_ge(q["xT_ready"], k.n + 1)
                        wait(eng, q["qk_copied"], k.n)
                        for i, w in enumerate((WQ, WK)):
                            mm = eng.matmul(halves(QK_BANK, S)[:, i, :], wT[:, w, :], xT[:, s, 1:1 + S],
                                            start=True, stop=True)
                        mm.then_inc(q["qk_ready"], 1)
                        wait(eng, q["v_copied"], k.n)
                        for c in range(J):
                            mm = eng.matmul(halves(V_BANK)[:, c, :], xT[:, s, 1 + c * P:1 + (c + 1) * P], wT[:, WV, :],
                                            start=True, stop=True)
                        mm.then_inc(q["v_ready"], 1)
                    if t.within(NB):
                        eng.wait_ge(q["xn_ready"], t.n + 1)
                        wait(eng, q["xT_ready"], t.n)
                        for j in range(J):
                            mm = eng.transpose(halves(T_BANK)[:, j, :], xn[:, t.parity, j, :], ident[:, :])
                        mm.then_inc(q["t_ready"], 1)
                    if o.within(NB):
                        s = o.parity
                        eng.wait_ge(q["pT_copied"], o.n + 1)
                        eng.wait_ge(q["v_copied"], o.n + 1)
                        wait(eng, q["o_copied"], o.n)
                        for j in range(J):
                            for c in range(J):
                                mm = eng.matmul(halves(O_BANK)[:, j, :], probT[:, s, c, j * P:(j + 1) * P],
                                                vrow[:, s, c, :], start=(c == 0), stop=(c == J - 1))
                        mm.then_inc(q["o_ready"], 1)
                run_steps(eng, NB, LAG, step)

            def act(eng):
                layer_consts_act(eng, layer)

                def step(t):
                    if t.within(NB):
                        s = t.parity
                        eng.wait_ge(q["t_ready"], t.n + 1)
                        wait(eng, q["v_ready"], t.n - 1)
                        eng.copy(xT[:, s, 1:1 + S].rearrange("c (p j) -> c j p", j=J),
                                 halves(T_BANK)).then_inc(q["xT_ready"], 1)
                    s_ = t.back(2)
                    if s_.within(NB):
                        s = s_.parity
                        eng.wait_ge(q["bias_ready"], s_.n + 1)
                        wait(eng, q["pT_ready"], s_.n - 1)
                        for j in range(J):
                            eng.activation(prob[:, s, j, :], halves(S_BANK, S)[:, j, :], ACT.Exp,
                                           bias=nmax_s[:, s, j:j + 1], scale=ATTN0_SCALE,
                                           accum_out=den[:, s, j:j + 1]).then_inc(q["exp_ready"], 1)
                    k = t.back(1)
                    if k.within(NB):
                        s = k.parity
                        eng.wait_ge(q["qk_ready"], k.n + 1)
                        wait(eng, q["s_ready"], k.n - 1)
                        eng.copy(qk[:, s, :, :], halves(QK_BANK, S)).then_inc(q["qk_copied"], 1)
                        eng.wait_ge(q["v_ready"], k.n + 1)
                        wait(eng, q["o_ready"], k.n - 1)
                        eng.copy(vrow[:, s, :, :], halves(V_BANK)).then_inc(q["v_copied"], 1)
                run_steps(eng, NB, LAG, step)

            def dve(eng):
                def step(t):
                    if t.within(NB):
                        wait(eng, q["t_ready"], t.n - 1)
                        normalise(eng, xn[:, t.parity], t.n).then_inc(q["xn_ready"], 1)
                    y = t.back(4)
                    if y.within(NB):
                        eng.wait_ge(q["y_ready"], y.n + 1)
                        eng.wait_ge(q["xb_ready"], y.n + 1)
                        eng.tensor_tensor(seq(y.n), seq(y.n), halves(Y_BANK), ALU.add).then_inc(q["updated"], 1)
                    s_ = t.back(2)
                    if s_.within(NB):
                        s = s_.parity
                        eng.wait_ge(q["s_ready"], s_.n + 1)
                        eng.tensor_reduce(nmax[:, s, :], halves(S_BANK, S), AX_X, ALU.max,
                                          negate=True).then_inc(q["max_ready"], 1)
                        eng.wait_ge(q["max_ready"], s_.n + 1)
                        wait(eng, q["exp_ready"], J * (s_.n - 1))
                        eng.tensor_scalar(nmax_s[:, s, :], nmax[:, s, :], ATTN0_SCALE, None,
                                          ALU.mult).then_inc(q["bias_ready"], 1)
                    o = t.back(3)
                    if o.within(NB):
                        s = o.parity
                        eng.wait_ge(q["pT_ready"], o.n + 1)
                        wait(eng, q["o_ready"], o.n - 1)
                        eng.tensor_copy(probT[:, s, :, :], halves(PT_BANK, S)).then_inc(q["pT_copied"], 1)
                        eng.reciprocal(rden[:, s, :], den[:, s, :]).then_inc(q["den_ready"], 1)
                    if y.within(NB):
                        eng.wait_ge(q["updated"], y.n + 1)
                        add_stats(eng, y.n, q["stats"])
                    if o.within(NB):
                        s = o.parity
                        eng.wait_ge(q["den_ready"], o.n + 1)
                        eng.wait_ge(q["o_ready"], o.n + 1)
                        wait(eng, q["y_ready"], o.n - 1)
                        eng.tensor_tensor(orow[:, s, :, :], halves(O_BANK),
                                          rden[:, s, :].unsqueeze(2).to_broadcast([P, J, C]),
                                          ALU.mult).then_inc(q["o_copied"], 1)
                run_steps(eng, NB, LAG, step)
                eng.wait_ge(q["stats"], J * NB)

            return pool, pe, act, dve

        def tern_layer(layer, last):
            names = "xn_ready t_ready xT_ready y_ready updated stats xb_ready".split()
            q = {n: sem(f"t{layer}_{n}") for n in names}
            LAG = 4

            def pool(eng):
                eng.wait_ge(ln_ready, layer + 1)

                def step(t):
                    if t.within(NB):
                        eng.wait_ge(q["xn_ready"], t.n + 1)
                        eng.tensor_tensor(seq(t.n), seq(t.n), btern_b[:, :, :], ALU.add).then_inc(q["xb_ready"], 1)
                run_steps(eng, NB, LAG, step)

            def pe(eng):
                def step(t):
                    k = t.back(1)
                    if k.within(NB):
                        s = k.parity
                        eng.wait_ge(q["xT_ready"], k.n + 1)
                        wait(eng, q["updated"], k.n - 1)
                        for j in range(J):
                            mm = eng.matmul(halves(2 + s)[:, j, :], xT[:, s, 1 + j * P:1 + (j + 1) * P], wT[:, TW, :],
                                            start=True, stop=True)
                        mm.then_inc(q["y_ready"], 1)
                    if t.within(NB):
                        eng.wait_ge(q["xn_ready"], t.n + 1)
                        wait(eng, q["xT_ready"], t.n - 1)
                        for j in range(J):
                            mm = eng.transpose(halves(t.parity)[:, j, :], xn[:, t.parity, j, :], ident[:, :])
                        mm.then_inc(q["t_ready"], 1)
                run_steps(eng, NB, LAG, step)

            def act(eng):
                layer_consts_act(eng, layer)

                def step(t):
                    if t.within(NB):
                        eng.wait_ge(q["t_ready"], t.n + 1)
                        wait(eng, q["y_ready"], t.n - 1)
                        eng.copy(xT[:, t.parity, 1:1 + S], banks[t.parity][:, 0:S]).then_inc(q["xT_ready"], 1)
                run_steps(eng, NB, LAG, step)

            def dve(eng):
                def step(t):
                    k = t.back(1)
                    if t.within(NB):
                        wait(eng, q["t_ready"], t.n - 1)
                        normalise(eng, xn[:, t.parity], t.n).then_inc(q["xn_ready"], 1)
                    if k.within(NB):
                        eng.wait_ge(q["y_ready"], k.n + 1)
                        eng.wait_ge(q["xb_ready"], k.n + 1)
                        eng.tensor_tensor(seq(k.n), seq(k.n), halves(2 + k.parity), ALU.add).then_inc(q["updated"], 1)
                    if not last:
                        d = t.back(2)
                        if d.within(NB):
                            eng.wait_ge(q["updated"], d.n + 1)
                            add_stats(eng, d.n, q["stats"])
                run_steps(eng, NB, LAG, step)
                if not last:
                    eng.wait_ge(q["stats"], J * NB)

            def sync(eng):
                if last:
                    for b in range(0, NB, LOAD):
                        eng.wait_ge(q["updated"], b + LOAD)
                        eng.dma_start(xout_v[:, b:b + LOAD, :], x_flat[:, b:b + LOAD, :]).then_inc(stored, 16)
                    eng.wait_ge(stored, 16 * (NB // LOAD))

            return pool, pe, act, dve, sync

        wqk_ones = sb("wqk_hi", [P, 2, H * D], F32R)
        wqk_parts = sb("wqk_lo", [P, 2, H * D], F32R)
        wv_hi = sb("wv_hi", [P, H * D], F32R)
        wv_lo = sb("wv_lo", [P, H * D], F32R)
        w1_raw = sb("w1_raw", [P, 512])
        wout = sb("wout", [P, PAIRS, C])
        bqk = sb("bqk", [P, 2, PAIRS])
        bv_b = sb("bv_b", [P, H * D])
        pos = sb("pos", [P, S])
        x_hi = sb("x_hi", [P, S], F32R)
        x_lo = sb("x_lo", [P, S], F32R)
        q_twice = sb("q_twice", [P, 2, 2, PG, S], F32R)
        q_rest = sb("q_rest", [P, 2, 2, PG, S], F32R)
        k_ones = sb("k_ones", [P, 2, 2, PG, S], F32R)
        k_parts = sb("k_parts", [P, 2, 2, PG, S], F32R)
        k_sum = sb("k_sum", [P, 2, S])
        v1 = sb("v1", [P, 2, J, HG, VW])
        nm1 = sb("nm1", [P, 2, 2 * PG * J])
        m_rows = sb("m_rows", [2 * PG * J, 2, P], F32R)
        p1 = sb("p1", [P, 2, J, S])
        rden1 = sb("rden1", [P, 2, J])
        o1 = tile(0, [2, J, HG, D])
        o1T = tile(4, [PAIRS, S])

        w1_loaded = sem("w1_loaded")
        w1_slice = sem("w1_slice_loaded")
        w1_split = sem("w1_split")
        attn1_ready = sem("attn1_consts_ready")
        bqk_scaled = sem("bqk_scaled")

        def attn1_setup_sync(sp):
            sp.dma_start(wout[:, :, :], W_out1.rearrange("(i p) e -> p i e", p=P)).then_inc(w1_loaded, 16)
            sp.dma_start(pos[0:D, :], pos_t).then_inc(w1_loaded, 16)
            sp.dma_start(pos[D:P, :], pos_t).then_inc(w1_loaded, 16)
            for i in range(2):
                for pr in range(PAIRS):
                    at = i * H * D + pr * P
                    sp.dma_start(bqk[:, i, pr:pr + 1],
                                 b_qkv1[at:at + P].rearrange("(c o) -> c o", o=1)).then_inc(w1_loaded, 16)
            sp.dma_start(bv_b[:, :], b_qkv1[2 * H * D:3 * H * D].rearrange("(o c) -> o c", o=1)
                         .to_broadcast([P, H * D])).then_inc(w1_loaded, 16)
            for k in range(6):
                wait(sp, w1_split, 2 * k)
                sp.dma_start(w1_raw[:, :], W_qkv1[:, k * 512:(k + 1) * 512]).then_inc(w1_slice, 16)

        def attn1_setup_dve(dve):
            dve.wait_ge(w1_loaded, 16 * (3 + 2 * PAIRS + 1))
            dve.tensor_scalar(bqk[:, 0, :], bqk[:, 0, :], 0.125, None, ALU.mult).then_inc(bqk_scaled, 1)
            for k in range(6):
                dve.wait_ge(w1_slice, 16 * (k + 1))
                part = slice((k % 2) * 512, (k % 2 + 1) * 512)
                hi, lo = ((wqk_ones[:, k // 2, part], wqk_parts[:, k // 2, part]) if k < 4
                          else (wv_hi[:, part], wv_lo[:, part]))
                f = 0.125 if k < 2 else 1.0
                dve.tensor_scalar(hi, w1_raw[:, :], f, None, ALU.mult).then_inc(w1_split, 1)
                dve.wait_ge(w1_split, 2 * k + 1)
                dve.scalar_tensor_tensor(out=lo, in0=w1_raw[:, :], scalar=f, in1=hi.bitcast(F32),
                                         op0=ALU.mult, op1=ALU.subtract).then_inc(w1_split, 1)
            dve.wait_ge(w1_split, 12)

        def attn1_setup_pool(pool):
            for tile in (q_rest, k_ones):
                pool.memset(tile[:, :, :, :, :].bitcast(F32), 0.0).then_inc(attn1_ready, 1)
            pool.memset(v1[:, :, :, :, D:VW], 1.0).then_inc(attn1_ready, 1)
            pool.wait_ge(attn1_ready, 3)
            pool.memset(k_ones[D:D + 1, :, 0, :, :].bitcast(F32), 1.0).then_inc(attn1_ready, 1)
            pool.wait_ge(attn1_ready, 4)
            pool.memset(k_ones[0:1, :, 1, :, :].bitcast(F32), 1.0).then_inc(attn1_ready, 1)
            pool.wait_ge(attn1_ready, N_ATTN1_READY)
        N_ATTN1_READY = 2 + 1 + 2
        N_UNITS = NB * G

        def attn1_layer(layer):
            names = ("xn_ready t_ready x_hi_ready x_lo_ready k_ready q_ready q_again_ready k_again_ready q_hi_ready q_lo_ready k_sum_ready k_hi_ready "
                     "k_lo_ready v_ready v_copied max_scored max_ready mT_ready mT_copied m_placed scores_ready "
                     "exp_ready pv_ready rden_ready o_copied oT_ready oT_copied y_ready updated stats xb_ready").split()
            q = {n: sem(f"b_{n}") for n in names}
            LAG = 4
            Q_BANK, K_BANK, MAX_BANK, MISC, S_BANK, O_BANK = 0, 1, 2, 3, (4, 5), (6, 7)
            HALF = (slice(0, D), slice(D, P))

            def pe(eng):
                def scores(u, h):
                    s, par, i = u.parity, h % 2, h // 2
                    if h == 0:
                        eng.wait_ge(q["m_placed"], 32 * (u.n + 1))
                        eng.wait_ge(q["k_lo_ready"], HG * (u.n + 1))
                        eng.wait_ge(q["q_lo_ready"], HG * (u.n + 1))
                    wait(eng, q["exp_ready"], HG * u.n + h - 1)
                    for c in range(J):
                        keys = slice(c * P, (c + 1) * P)
                        out = halves(S_BANK[par], S)[:, c, :]
                        eng.matmul(out, k_parts[:, s, par, i, keys], q_twice[:, s, par, i, :], start=True, stop=False)
                        mm = eng.matmul(out, k_ones[:, s, par, i, keys], q_rest[:, s, par, i, :], start=False, stop=True)
                    mm.then_inc(q["scores_ready"], 1)

                def project(u, i):
                    pr = u.parity * PG + i
                    if i == 0:
                        eng.wait_ge(q["x_lo_ready"], u.half + 1)
                    wait(eng, q["k_sum_ready"], PG * u.n + i)
                    for z, bank in ((1, K_BANK), (0, Q_BANK)):
                        if z == 0:
                            wait(eng, q["q_lo_ready"], HG * u.n + 2 * i)
                        out = banks[bank][:, 0:S]
                        hi, lo = wqk_ones[:, z, pr * P:(pr + 1) * P], wqk_parts[:, z, pr * P:(pr + 1) * P]
                        eng.matmul(out, hi, x_hi[:, :], start=True, stop=False)
                        eng.matmul(out, hi, x_lo[:, :], start=False, stop=False)
                        eng.matmul(out, lo, x_hi[:, :], start=False,
                                   stop=True).then_inc(q["k_ready"] if z else q["q_ready"], 1)

                def values(u, j):
                    cols = slice(u.parity * HG * D, (u.parity + 1) * HG * D)
                    if j == 0:
                        eng.wait_ge(q["x_lo_ready"], u.half + 1)
                    out = banks[MISC][:, :]
                    toks = slice(j * P, (j + 1) * P)
                    eng.matmul(out, x_hi[:, toks], wv_hi[:, cols], start=True, stop=False)
                    eng.matmul(out, x_hi[:, toks], wv_lo[:, cols], start=False, stop=False)
                    eng.matmul(out, x_lo[:, toks], wv_hi[:, cols], start=False, stop=True).then_inc(q["v_ready"], 1)

                def row_max(u, h):
                    s, par, i = u.parity, h % 2, h // 2
                    eng.wait_ge(q["q_again_ready"], HG * u.n + h + 1)
                    eng.wait_ge(q["k_again_ready"], HG * u.n + h + 1)
                    eng.wait_ge(q["k_lo_ready"], HG * u.n + h + 1)
                    wait(eng, q["max_ready"], HG * u.n + h)
                    for j in range(J):
                        mm = eng.matmul(halves(MAX_BANK, S)[:, j, :], q_twice[:, s, par, i, j * P:(j + 1) * P],
                                        k_parts[:, s, par, i, :], start=True, stop=True)
                    mm.then_inc(q["max_scored"], 1)

                def weigh(u, h):
                    s, par = u.parity, h % 2
                    eng.wait_ge(q["exp_ready"], HG * u.n + h + 1)
                    if h == 0:
                        eng.wait_ge(q["v_copied"], J * (u.n + 1))
                    wait(eng, q["o_copied"], HG * u.n + h - 1)
                    for j in range(J):
                        for c in range(J):
                            mm = eng.matmul(halves(O_BANK[par], VW)[:, j, :], p1[:, par, c, j * P:(j + 1) * P],
                                            v1[:, s, c, h, :], start=(c == 0), stop=(c == J - 1))
                    mm.then_inc(q["pv_ready"], 1)

                def turn_out(u, r):
                    eng.wait_ge(q["o_copied"], HG * (u.n + 1))
                    for i in range(2):
                        for j in range(J):
                            mm = eng.transpose(banks[MISC][:, (i * J + j) * P:(i * J + j + 1) * P],
                                               o1[:, u.parity, j, 4 * r + 2 * i:4 * r + 2 * i + 2, :]
                                               .rearrange("p h d -> p (h d)"), ident[:, :])
                    mm.then_inc(q["oT_ready"], 1)

                def step(t):
                    a, b, c = t.back(1), t.back(2), t.back(3)
                    for s in range(HG):
                        if s > 0 and b.within(N_UNITS):
                            scores(b, s)
                        if s < PG and a.within(N_UNITS):
                            project(a, s)
                        if 2 <= s < 6 and a.within(N_UNITS):
                            row_max(a, 2 * (s - 2) + 1)
                        if s == 0:
                            if c.within(N_UNITS):
                                weigh(c, HG - 1)
                            if a.within(N_UNITS):
                                wait(eng, q["mT_copied"], a.n)
                                values(a, 0)
                            if b.within(N_UNITS):
                                scores(b, 0)
                        if s == 1 and c.within(N_UNITS):
                            if a.within(N_UNITS):
                                eng.wait_ge(q["v_copied"], J * a.n + 1)
                            turn_out(c, 0)
                        if s == 2 and a.within(N_UNITS):
                            if c.within(N_UNITS):
                                eng.wait_ge(q["oT_copied"], 2 * c.n + 1)
                            else:
                                eng.wait_ge(q["v_copied"], J * a.n + 1)
                            values(a, 1)
                        if s == 3 and c.within(N_UNITS):
                            if a.within(N_UNITS):
                                eng.wait_ge(q["v_copied"], J * (a.n + 1))
                            else:
                                eng.wait_ge(q["oT_copied"], 2 * c.n + 1)
                            turn_out(c, 1)
                        if s == 4 and t.parity == 0 and c.within(N_UNITS):
                            eng.wait_ge(q["oT_copied"], 4 * (c.half + 1))
                            for j in range(J):
                                for i in range(PAIRS):
                                    mm = eng.matmul(halves(MISC)[:, j, :], o1T[:, i, j * P:(j + 1) * P],
                                                    wout[:, i, :], start=(i == 0), stop=(i == PAIRS - 1))
                            mm.then_inc(q["y_ready"], 1)
                        if s == 6 and a.within(N_UNITS):
                            eng.wait_ge(q["max_ready"], HG * (a.n + 1))
                            if t.parity == 0 and c.within(N_UNITS):
                                eng.wait_ge(q["updated"], c.half + 1)
                            elif c.within(N_UNITS):
                                eng.wait_ge(q["oT_copied"], 2 * (c.n + 1))
                            else:
                                eng.wait_ge(q["v_copied"], J * (a.n + 1))
                            eng.transpose(banks[MISC][0:2 * PG * J, 0:P], nm1[:, a.parity, :],
                                          ident[:, :]).then_inc(q["mT_ready"], 1)
                        if s == 7 and t.parity == 0 and t.within(N_UNITS):
                            eng.wait_ge(q["xn_ready"], t.half + 1)
                            if a.within(N_UNITS):
                                eng.wait_ge(q["mT_copied"], a.n + 1)
                            for j in range(J):
                                mm = eng.transpose(halves(MISC)[:, j, :], xn[:, 0, j, :], ident[:, :])
                            mm.then_inc(q["t_ready"], 1)
                        if s >= 1 and b.within(N_UNITS):
                            weigh(b, s - 1)
                        if 1 <= s < 5 and a.within(N_UNITS):
                            row_max(a, 2 * (s - 1))
                    if t.parity == 0 and t.within(N_UNITS):
                        eng.wait_ge(q["x_lo_ready"], t.half + 1)
                run_steps(eng, N_UNITS, LAG, step)

            def act(eng):
                layer_consts_act(eng, layer)
                eng.wait_ge(attn1_ready, N_ATTN1_READY)
                eng.wait_ge(bqk_scaled, 1)

                def exp(u, h):
                    eng.wait_ge(q["scores_ready"], HG * u.n + h + 1)
                    wait(eng, q["pv_ready"], HG * u.n + h - 1)
                    eng.activation(p1[:, h % 2, :, :], halves(S_BANK[h % 2], S), ACT.Exp).then_inc(q["exp_ready"], 1)

                def step(t):
                    a, b, c = t.back(1), t.back(2), t.back(3)
                    for s in range(HG):
                        if s > 0 and b.within(N_UNITS):
                            exp(b, s)
                        if s < PG and a.within(N_UNITS):
                            pr = a.parity * PG + s
                            eng.wait_ge(q["q_ready"], PG * a.n + s + 1)
                            for par in range(2):
                                r = HALF[par]
                                eng.activation(q_twice[r, a.parity, par, s, :], banks[Q_BANK][r, 0:S],
                                               ACT.Identity, bias=bqk[r, 0, pr:pr + 1]).then_inc(q["q_hi_ready"], 1)
                            eng.wait_ge(q["k_sum_ready"], PG * a.n + s + 1)
                            for par in range(2):
                                r = HALF[par]
                                eng.copy(k_ones[r, a.parity, par, s, :], k_sum[r, s % 2, :]).then_inc(q["k_hi_ready"], 1)
                            for par in range(2):
                                r = HALF[par]
                                eng.wait_ge(q["q_hi_ready"], HG * a.n + 2 * s + par + 1)
                                eng.copy(q_twice[HALF[1 - par], a.parity, par, s, :],
                                         q_twice[r, a.parity, par, s, :].bitcast(F32)).then_inc(q["q_again_ready"], 1)
                        if s == 0 and b.within(N_UNITS):
                            exp(b, 0)
                        if s in (1, 3) and c.within(N_UNITS):
                            rnd = s // 2
                            eng.wait_ge(q["oT_ready"], 2 * c.n + rnd + 1)
                            if c.parity == 0:
                                wait(eng, q["y_ready"], c.half)
                            at = c.parity * PG + 2 * rnd
                            eng.copy(o1T[:, at:at + 2, :], halves(MISC, S)).then_inc(q["oT_copied"], 1)
                        if s == 7 and t.parity == 0 and t.within(N_UNITS):
                            eng.wait_ge(q["t_ready"], t.half + 1)
                            eng.copy(x_hi[:, :], banks[MISC][:, 0:S]).then_inc(q["x_hi_ready"], 1)
                run_steps(eng, N_UNITS, LAG, step)

            def dve(eng):
                eng.wait_ge(attn1_ready, N_ATTN1_READY)
                eng.wait_ge(bqk_scaled, 1)

                def norm(u, h):
                    s, par = u.parity, h % 2
                    eng.wait_ge(q["pv_ready"], HG * u.n + h + 1)
                    wait(eng, q["o_copied"], HG * u.n + h - 1)
                    eng.reciprocal(rden1[:, par, :], halves(O_BANK[par], VW)[:, :, D]).then_inc(q["rden_ready"], 1)
                    eng.wait_ge(q["rden_ready"], HG * u.n + h + 1)
                    if h == 0:
                        wait(eng, q["oT_ready"], 2 * (u.n - 1))
                    eng.tensor_tensor(o1[:, s, :, h, :], halves(O_BANK[par], VW)[:, :, 0:D],
                                      rden1[:, par, :].unsqueeze(2).to_broadcast([P, J, D]),
                                      ALU.mult).then_inc(q["o_copied"], 1)

                def copy_values(u, j):
                    cols = slice(u.parity * HG * D, (u.parity + 1) * HG * D)
                    eng.wait_ge(q["v_ready"], J * u.n + j + 1)
                    eng.tensor_tensor(v1[:, u.parity, j, :, 0:D], banks[MISC][:, :].rearrange("p (h d) -> p h d", d=D),
                                      bv_b[:, cols].rearrange("p (h d) -> p h d", d=D), ALU.add).then_inc(q["v_copied"], 1)

                def reduce(u, h):
                    par, i = h % 2, h // 2
                    at = par * PG * J + i * J
                    eng.wait_ge(q["max_scored"], HG * u.n + h + 1)
                    if h == 0:
                        wait(eng, q["mT_ready"], u.n - 1)
                    eng.tensor_reduce(nm1[:, u.parity, at:at + J], halves(MAX_BANK, S), AX_X, ALU.max,
                                      negate=True).then_inc(q["max_ready"], 1)

                def step(t):
                    a, b, c = t.back(1), t.back(2), t.back(3)
                    for s in range(HG):
                        if 2 <= s < 6 and a.within(N_UNITS):
                            reduce(a, 2 * (s - 2))
                        if s == 5 and t.parity == 0 and t.within(N_UNITS):
                            wait(eng, q["t_ready"], t.half)
                            normalise(eng, xn[:, 0], t.half).then_inc(q["xn_ready"], 1)
                        if s < PG and a.within(N_UNITS):
                            pr = a.parity * PG + s
                            eng.wait_ge(q["k_ready"], PG * a.n + s + 1)
                            wait(eng, q["k_lo_ready"], HG * a.n + 2 * (s - 1))
                            eng.scalar_tensor_tensor(out=k_sum[:, s % 2, :], in0=banks[K_BANK][:, 0:S],
                                                     scalar=bqk[:, 1, pr:pr + 1], in1=pos[:, :], op0=ALU.add,
                                                     op1=ALU.add).then_inc(q["k_sum_ready"], 1)
                        if 2 <= s < 6 and a.within(N_UNITS):
                            reduce(a, 2 * (s - 2) + 1)
                        if s == 0 and c.within(N_UNITS):
                            norm(c, HG - 1)
                        if s < PG and a.within(N_UNITS):
                            for par in range(2):
                                r = HALF[par]
                                eng.wait_ge(q["q_hi_ready"], HG * a.n + 2 * s + par + 1)
                                eng.scalar_tensor_tensor(out=q_rest[r, a.parity, par, s, :], in0=banks[Q_BANK][r, 0:S],
                                                         scalar=bqk[r, 0, pr:pr + 1],
                                                         in1=q_twice[r, a.parity, par, s, :].bitcast(F32),
                                                         op0=ALU.add, op1=ALU.subtract).then_inc(q["q_lo_ready"], 1)
                        if s in (0, 2) and a.within(N_UNITS):
                            copy_values(a, s // 2)
                        if s < PG and a.within(N_UNITS):
                            for par in range(2):
                                eng.wait_ge(q["k_hi_ready"], HG * a.n + 2 * s + par + 1)
                                eng.tensor_copy(k_parts[HALF[1 - par], a.parity, par, s, :],
                                                k_ones[HALF[par], a.parity, par, s, :].bitcast(F32)
                                                ).then_inc(q["k_again_ready"], 1)
                        if s == 4 and t.parity == 0 and c.within(N_UNITS):
                            eng.wait_ge(q["y_ready"], c.half + 1)
                            eng.wait_ge(q["xb_ready"], c.half + 1)
                            eng.tensor_tensor(seq(c.half), seq(c.half), halves(MISC), ALU.add).then_inc(q["updated"], 1)
                            eng.wait_ge(q["updated"], c.half + 1)
                            add_stats(eng, c.half, q["stats"])
                        if s == 6 and a.within(N_UNITS):
                            eng.wait_ge(q["mT_ready"], a.n + 1)
                            wait(eng, q["m_placed"], 32 * (a.n - 1))
                            eng.tensor_copy(m_rows[:, a.parity, :], banks[MISC][0:2 * PG * J, 0:P]).then_inc(q["mT_copied"], 1)
                        if s == 7 and t.parity == 0 and t.within(N_UNITS):
                            eng.wait_ge(q["x_hi_ready"], t.half + 1)
                            eng.tensor_tensor(x_lo[:, :], banks[MISC][:, 0:S], x_hi[:, :].bitcast(F32),
                                              ALU.subtract).then_inc(q["x_lo_ready"], 1)
                        if s >= 1 and b.within(N_UNITS):
                            norm(b, s - 1)
                run_steps(eng, N_UNITS, LAG, step)
                eng.wait_ge(q["stats"], J * NB)

            def pool(eng):
                eng.wait_ge(ln_ready, layer + 1)

                def step(t):
                    a = t.back(1)
                    if a.within(N_UNITS):
                        for s in range(PG):
                            for par in range(2):
                                r = HALF[par]
                                eng.wait_ge(q["k_hi_ready"], HG * a.n + 2 * s + par + 1)
                                wait(eng, q["k_lo_ready"], HG * a.n + 2 * s + par)
                                eng.tensor_tensor(k_parts[r, a.parity, par, s, :], k_sum[r, s % 2, :],
                                                  k_ones[r, a.parity, par, s, :].bitcast(F32),
                                                  ALU.subtract).then_inc(q["k_lo_ready"], 1)
                    if t.parity == 0 and t.within(N_UNITS):
                        if a.within(N_UNITS):
                            eng.wait_ge(q["k_lo_ready"], HG * (a.n + 1))
                        eng.wait_ge(q["xn_ready"], t.half + 1)
                        eng.tensor_tensor(seq(t.half), seq(t.half), bout_b[:, :, :], ALU.add).then_inc(q["xb_ready"], 1)
                run_steps(eng, N_UNITS, LAG, step)

            def sync(eng):
                def step(t):
                    a = t.back(1)
                    if a.within(N_UNITS):
                        eng.wait_ge(q["mT_copied"], a.n + 1)
                        for par, row in ((0, D), (1, 0)):
                            eng.dma_start(q_rest[row:row + 1, a.parity, par, :, :].bitcast(F32)
                                          .rearrange("o i (j p) -> o (i j) p", j=J),
                                          m_rows[par * PG * J:(par + 1) * PG * J, a.parity, :].bitcast(F32)
                                          ).then_inc(q["m_placed"], 16)
                run_steps(eng, N_UNITS, LAG, step)

            return pool, pe, act, dve, sync

        ffn_a = ffn_layer(0)
        attn_b = attn0_layer(1)
        ffn_c = ffn_layer(2)
        tern_d = tern_layer(3, last=False)
        attn_e = attn1_layer(4)
        tern_f = tern_layer(5, last=True)
        layers = (ffn_a, attn_b, ffn_c, tern_d, attn_e, tern_f)

        block = ctx.enter_context(nc.Block())

        @block.sync
        def _(sp):
            setup_sync(sp)
            attn1_setup_sync(sp)
            attn_e[4](sp)
            tern_f[4](sp)

        @block.gpsimd
        def _(pool):
            setup_pool(pool)
            attn1_setup_pool(pool)
            for layer in layers:
                layer[0](pool)

        @block.tensor
        def _(pe):
            setup_pe(pe)
            for layer in layers:
                layer[1](pe)

        @block.scalar
        def _(act):
            for layer in layers:
                layer[2](act)

        @block.vector
        def _(dve):
            setup_dve(dve)
            for layer in layers:
                if layer is attn_e:
                    attn1_setup_dve(dve)
                layer_consts_dve(dve)
                layer[3](dve)


_INS = ['L0_attn_x', 'L0_attn_w_qkv', 'L0_attn_w_proj', 'L0_attn_b_proj', 'L0_ffn_W_r', 'L0_ffn_W_k', 'L0_ffn_W_v',
        'L0_ffn_mu_r', 'L0_ffn_mu_k', 'L1_attn_W_qkv', 'L1_attn_b_qkv', 'L1_attn_W_out', 'L1_attn_b_out',
        'L1_ffn_weight', 'L1_ffn_alpha', 'L1_ffn_bias']


def position_table():
    positions = np.arange(S, dtype=np.float32)[:, None]
    div = np.exp(np.arange(0, D, 2, dtype=np.float32) * np.float32(-(np.log(10000.0) / D)))
    table = np.zeros((S, D), np.float32)
    table[:, 0::2] = np.sin(positions * div)
    table[:, 1::2] = np.cos(positions * div)
    return np.ascontiguousarray(table.reshape(P, J, D).transpose(2, 1, 0).reshape(D, S))


def kernel(**inputs):
    import concourse.bacc as _bacc
    from concourse.bass_utils import run_bass_kernel_spmd as _run

    nc = _bacc.Bacc("TRN2", target_bir_lowering=False, num_devices=1)
    arrays, args = {}, []
    for name in _INS:
        a = np.ascontiguousarray(inputs[name])
        arrays[f"in_{name}"] = a
        args.append(nc.dram_tensor(f"in_{name}", a.shape, mybir.dt.from_np(a.dtype), kind="ExternalInput").ap())
    arrays["position_table"] = position_table()
    args.append(nc.dram_tensor("position_table", (D, S), F32, kind="ExternalInput").ap())
    args.append(nc.dram_tensor("out", (NB, S, C), F32, kind="ExternalOutput").ap())
    macaron_kernel(nc, *args)
    r = _run(nc, [arrays], core_ids=[0])
    return r.results[0]["out"]
```

```python
from contextlib import ExitStack

import numpy as np

import concourse.bass as bass
from concourse import mybir

F32 = mybir.dt.float32
F32R = mybir.dt.float32r
ALU = mybir.AluOpType
ACT = mybir.ActivationFunctionType
AX_X = mybir.AxisListType.X

P = 128
NB, S, C = 32, 256, 128
J = S // P
H, D = 16, 64
PAIRS = H // 2
G = 2
HG = H // G
PG = PAIRS // G
VW = 96
ATTN0_SCALE = float(1.0 / np.sqrt(8.0).astype(np.float32))
EPS = 1e-5
LOAD = 4


class Step:

    def __init__(self, half, parity):
        self.half, self.parity = half, parity

    def back(self, lag):
        n = self.parity - lag
        return Step(self.half + (n - n % 2) // 2, n % 2)

    @property
    def n(self):
        return self.half * 2 + self.parity

    def within(self, count):
        return not isinstance(self.half, int) or 0 <= self.n < count


def run_steps(eng, count, lag, step):
    for t in range(lag):
        step(Step(t // 2, t % 2))
    with eng.Fori(lag // 2, count // 2) as half:
        step(Step(half, 0))
        step(Step(half, 1))
    for t in range(count, count + lag):
        step(Step(t // 2, t % 2))


def wait(eng, sem, value):
    if isinstance(value, int) and value <= 0:
        return
    eng.wait_ge(sem, value)


def macaron_kernel(nc, x_in, w_qkv0, w_proj0, b_proj0, W_r, W_k, W_v, mu_r, mu_k,
                   W_qkv1, b_qkv1, W_out1, b_out1, w_tern, alpha, bias_tern, pos_t, x_out):
    ctx = ExitStack()
    with ctx:
        def sb(name, shape, dt=F32):
            return ctx.enter_context(nc.sbuf_tensor(name, shape, dt))

        def sem(name):
            return ctx.enter_context(nc.semaphore(name))

        x = sb("x", [P, NB, J, C])
        ident = sb("ident", [P, P])
        ones = sb("ones", [P, P])
        stats = sb("stats", [P, NB * J, 6])
        rstd = sb("rstd", [P, NB * J])
        nbias = sb("nbias", [P, NB * J])
        lnt = sb("lnt", [P, 3, NB * J])

        w_raw = sb("w_raw", [P, 8, P])
        wT = sb("wT", [P, 8, P])
        WQ, WK, WV, WP, FR, FK, FV, TW = range(8)
        wr_now, wr_prev = sb("wr_now", [P, P]), sb("wr_prev", [P, P])
        wk_now, wk_prev = sb("wk_now", [P, P]), sb("wk_prev", [P, P])
        mu = sb("mu", [P, 4])
        bproj_b = sb("bproj_b", [P, J, C])
        bout_b = sb("bout_b", [P, J, C])
        btern_b = sb("btern_b", [P, J, C])
        alpha_b = sb("alpha_b", [P, 1])
        tern = sb("tern", [P, 4])
        ternm = sb("ternm", [P, P])

        xn = sb("xn", [P, 2, J, C])
        xT = sb("xT", [P, 2, 1 + S])

        banks = [ctx.enter_context(nc.psum_tensor(f"bank{i}", [P, 512], F32)) for i in range(8)]

        def halves(b, w=C):
            return banks[b][:, 0:J * w].rearrange("p (j c) -> p j c", j=J)

        block_entry = sem("consts_ready")
        loaded = [sem(f"x_loaded{i}") for i in range(NB // LOAD)]
        stored = sem("x_stored")
        w_loaded = sem("w_loaded")
        ident_zeroed = sem("ident_zeroed")
        wT_ready = sem("wT_ready")
        w_ready = sem("w_ready")
        chain = sem("dve_chain")
        ln_var = sem("ln_var")
        ln_std = sem("ln_std")
        ln_ready = sem("ln_ready")
        tern_sum = sem("tern_sum")

        xin_v = x_in.rearrange("b (p j) c -> p b (j c)", j=J)
        xout_v = x_out.rearrange("b (p j) c -> p b (j c)", j=J)
        x_flat = x[:, :, :, :].rearrange("p b j c -> p b (j c)")
        x_chunks = x[:, :, :, :].rearrange("p b j c -> p (b j) c")

        chain_count = [0]

        def chained(dve, ins):
            chain_count[0] += 1
            ins.then_inc(chain, 1)
            dve.wait_ge(chain, chain_count[0])

        def setup_sync(sp):
            for k in range(3):
                sp.dma_start(w_raw[:, WQ + k, :], w_qkv0[k * P:(k + 1) * P, :]).then_inc(w_loaded, 16)
            for k, w in ((WP, w_proj0), (FR, W_r), (FK, W_k), (FV, W_v), (TW, w_tern)):
                sp.dma_start(w_raw[:, k, :], w).then_inc(w_loaded, 16)
            sp.dma_start(mu[:, 0:1], mu_r.rearrange("(c o) -> c o", o=1)).then_inc(w_loaded, 16)
            sp.dma_start(mu[:, 1:2], mu_k.rearrange("(c o) -> c o", o=1)).then_inc(w_loaded, 16)
            for tile, b in ((bproj_b, b_proj0), (bout_b, b_out1), (btern_b, bias_tern)):
                row = b.rearrange("(o c) -> o c", o=1).to_broadcast([P, C])
                for j in range(J):
                    sp.dma_start(tile[:, j, :], row).then_inc(w_loaded, 16)
            sp.dma_start(alpha_b[:, :], alpha.rearrange("(o c) -> o c", o=1).to_broadcast([P, 1])).then_inc(w_loaded, 16)
            for b in range(0, NB, LOAD):
                sp.dma_start(x_flat[:, b:b + LOAD, :], xin_v[:, b:b + LOAD, :]).then_inc(loaded[b // LOAD], 16)

        N_WDMA = 3 + 5 + 2 + 3 * J + 1

        def setup_pool(pool):
            pool.memset(ident[:, :], 0.0).then_inc(ident_zeroed, 1)
            pool.wait_ge(ident_zeroed, 1)
            pool.affine_select(out=ident[:, :], in_=ident[:, :], compare_op=ALU.not_equal, fill=1.0, base=0,
                               pattern=[[-1, P]], channel_multiplier=1).then_inc(block_entry, 1)
            pool.memset(xT[:, :, 0:1], 0.0).then_inc(block_entry, 1)
            pool.memset(ones[:, :], 1.0).then_inc(block_entry, 1)

        def setup_pe(pe):
            pe.wait_ge(w_loaded, 16 * N_WDMA)
            pe.wait_ge(block_entry, 3)
            for k in range(8):
                mm = pe.transpose(banks[k // 4][:, (k % 4) * P:(k % 4 + 1) * P], w_raw[:, k, :], ident[:, :])
            mm.then_inc(wT_ready, 1)
            pe.wait_ge(tern_sum, 1)
            pe.matmul(banks[2][:, 0:1], ones[:, :], tern[:, 0:1], start=True, stop=True).then_inc(tern_sum, 1)

        def setup_dve(dve):
            dve.wait_ge(w_loaded, 16 * N_WDMA)
            dve.tensor_reduce(tern[:, 0:1], w_raw[:, TW, :], AX_X, ALU.add,
                              apply_absolute_value=True).then_inc(tern_sum, 1)
            dve.tensor_scalar(mu[:, 2:4], mu[:, 0:2], -1.0, 1.0, ALU.mult, ALU.add).then_inc(chain, 1)
            chain_count[0] += 1
            dve.wait_ge(wT_ready, 1)
            for half in range(2):
                dve.tensor_copy(wT[:, 4 * half:4 * half + 4, :],
                                banks[half][:, :].rearrange("p (k c) -> p k c", k=4)).then_inc(chain, 1)
                chain_count[0] += 1
            dve.wait_ge(chain, chain_count[0])
            for w, now, prev, m in ((FR, wr_now, wr_prev, 0), (FK, wk_now, wk_prev, 1)):
                dve.tensor_scalar(now[:, :], wT[:, w, :], mu[:, m:m + 1], None, ALU.mult).then_inc(w_ready, 1)
                dve.tensor_scalar(prev[:, :], wT[:, w, :], mu[:, 2 + m:3 + m], None, ALU.mult).then_inc(w_ready, 1)
            dve.tensor_scalar(wT[:, FV, :], wT[:, FV, :], 0.5, None, ALU.mult).then_inc(w_ready, 1)
            dve.tensor_scalar(btern_b[:, :, :], btern_b[:, :, :], 0.5, None, ALU.mult).then_inc(w_ready, 1)
            dve.wait_ge(tern_sum, 2)
            chained(dve, dve.tensor_scalar(tern[:, 1:2], banks[2][:, 0:1], 1.0 / (C * C), 0.7, ALU.mult, ALU.mult))
            chained(dve, dve.tensor_scalar(tern[:, 2:3], tern[:, 1:2], -1.0, None, ALU.mult))
            chained(dve, dve.tensor_scalar(ternm[:, :], wT[:, TW, :], tern[:, 2:3], None, ALU.is_lt))
            chained(dve, dve.scalar_tensor_tensor(out=wT[:, TW, :], in0=wT[:, TW, :], scalar=tern[:, 1:2],
                                                  in1=ternm[:, :], op0=ALU.is_gt, op1=ALU.subtract))
            dve.tensor_scalar(wT[:, TW, :], wT[:, TW, :], alpha_b[:, 0:1], 0.5, ALU.mult, ALU.mult).then_inc(w_ready, 1)
            for b in range(NB):
                if b % LOAD == 0:
                    dve.wait_ge(loaded[b // LOAD], 16)
                for j in range(J):
                    dve.bn_stats(stats[:, b * J + j, :], x[:, b, j, :]).then_inc(chain, 1)
                    chain_count[0] += 1

        N_WREADY = 7
        ln_done = [0]

        def layer_consts_dve(dve):
            k = ln_done[0]
            ln_done[0] += 1
            me, mo = stats[:, :, 1], stats[:, :, 4]
            m2e, m2o = stats[:, :, 2], stats[:, :, 5]
            a, b, c = lnt[:, 0, :], lnt[:, 1, :], lnt[:, 2, :]
            dve.wait_ge(chain, chain_count[0])
            chained(dve, dve.tensor_tensor(a, me, mo, ALU.subtract))
            chained(dve, dve.tensor_tensor(b, a, a, ALU.mult))
            chained(dve, dve.tensor_tensor(a, m2e, m2o, ALU.add))
            chained(dve, dve.tensor_scalar(a, a, 1.0 / C, EPS, ALU.mult, ALU.add))
            chained(dve, dve.scalar_tensor_tensor(out=c, in0=b, scalar=0.25, in1=a, op0=ALU.mult, op1=ALU.add))
            chained(dve, dve.tensor_tensor(b, me, mo, ALU.add))
            dve.tensor_copy(a, c).then_inc(ln_var, 1)
            dve.wait_ge(ln_std, k + 1)
            chained(dve, dve.reciprocal(a, rstd[:, :]))
            chained(dve, dve.tensor_tensor(nbias[:, :], a, a, ALU.mult))
            chained(dve, dve.tensor_tensor(nbias[:, :], nbias[:, :], c, ALU.mult))
            chained(dve, dve.tensor_scalar(nbias[:, :], nbias[:, :], -0.5, 1.5, ALU.mult, ALU.add))
            chained(dve, dve.tensor_tensor(rstd[:, :], a, nbias[:, :], ALU.mult))
            dve.scalar_tensor_tensor(out=nbias[:, :], in0=b, scalar=-0.5, in1=rstd[:, :],
                                     op0=ALU.mult, op1=ALU.mult).then_inc(ln_ready, 1)
            dve.wait_ge(ln_ready, k + 1)

        def layer_consts_act(act, k):
            act.wait_ge(ln_var, k + 1)
            act.activation(rstd[:, :], lnt[:, 0, :], ACT.Sqrt).then_inc(ln_std, 1)

        def normalise(eng, out, n):
            for j in range(J):
                at = n * J + j
                ins = eng.tensor_scalar(out[:, j, :], x_chunks[:, bass.ds(at, 1), :].rearrange("p o c -> p (o c)"),
                                        rstd[:, bass.ds(at, 1)], nbias[:, bass.ds(at, 1)], ALU.mult, ALU.add)
            return ins

        def add_stats(dve, n, sems):
            for j in range(J):
                at = n * J + j
                dve.bn_stats(stats[:, bass.ds(at, 1), :].rearrange("p o s -> p (o s)"),
                             x_chunks[:, bass.ds(at, 1), :].rearrange("p o c -> p (o c)")).then_inc(sems, 1)

        def seq(n):
            return x[:, bass.ds(n, 1), :, :].rearrange("p o j c -> p (o j) c")

        def ffn_layer(layer):
            xn_ready, t_ready, xT_ready = sem(f"f{layer}_xn_ready"), sem(f"f{layer}_t_ready"), sem(f"f{layer}_xT_ready")
            k_ready, r_ready = sem(f"f{layer}_k_ready"), sem(f"f{layer}_r_ready")
            relu_ready, gate_ready = sem(f"f{layer}_relu_ready"), sem(f"f{layer}_gate_ready")
            kact_ready, kv_ready = sem(f"f{layer}_kact_ready"), sem(f"f{layer}_kv_ready")
            gated, updated, done = sem(f"f{layer}_gated"), sem(f"f{layer}_updated"), sem(f"f{layer}_stats")
            LAG = 4
            T_BANK, K_BANK, R_BANK, KV_BANK = (0, 1), (2, 3), (4, 5), (6, 7)

            def pool(eng):
                pass

            def pe(eng):
                if layer == 0:
                    eng.wait_ge(w_ready, N_WREADY)

                def step(t):
                    v = t.back(2)
                    if v.within(NB):
                        s = v.parity
                        eng.wait_ge(kact_ready, v.n + 1)
                        wait(eng, gated, v.n - 1)
                        for j in range(J):
                            mm = eng.matmul(halves(KV_BANK[s])[:, j, :], kact[:, s, j::J], wT[:, FV, :],
                                            start=True, stop=True)
                        mm.then_inc(kv_ready, 1)
                    k = t.back(1)
                    if k.within(NB):
                        s = k.parity
                        eng.wait_ge(xT_ready, k.n + 1)
                        wait(eng, relu_ready, k.n - 1)
                        wait(eng, kact_ready, k.n - 1)
                        eng.matmul(banks[K_BANK[s]][:, 0:S], wk_now[:, :], xT[:, s, 1:1 + S], start=True, stop=False)
                        eng.matmul(banks[K_BANK[s]][:, 0:S], wk_prev[:, :], xT[:, s, 0:S], start=False,
                                   stop=True).then_inc(k_ready, 1)
                        wait(eng, gate_ready, k.n - 1)
                        for j in range(J):
                            eng.matmul(halves(R_BANK[s])[:, j, :], xT[:, s, 1 + j::J], wr_now[:, :],
                                       start=True, stop=False)
                            mm = eng.matmul(halves(R_BANK[s])[:, j, :], xT[:, s, j:S:J], wr_prev[:, :],
                                            start=False, stop=True)
                        mm.then_inc(r_ready, 1)
                    if t.within(NB):
                        eng.wait_ge(xn_ready, t.n + 1)
                        wait(eng, xT_ready, t.n - 1)
                        for j in range(J):
                            mm = eng.transpose(halves(T_BANK[t.parity])[:, j, :], xn[:, t.parity, j, :], ident[:, :])
                        mm.then_inc(t_ready, 1)
                run_steps(eng, NB, LAG, step)

            def act(eng):
                layer_consts_act(eng, layer)

                def step(t):
                    k = t.back(1)
                    if k.within(NB):
                        s = k.parity
                        eng.wait_ge(k_ready, k.n + 1)
                        wait(eng, kact_ready, k.n - 1)
                        eng.activation(relu[:, s, :], banks[K_BANK[s]][:, 0:S], ACT.Relu).then_inc(relu_ready, 1)
                        eng.wait_ge(r_ready, k.n + 1)
                        wait(eng, gated, k.n - 1)
                        eng.activation(gate[:, s, :, :], halves(R_BANK[s]), ACT.Sigmoid).then_inc(gate_ready, 1)
                    if t.within(NB):
                        s = t.parity
                        eng.wait_ge(t_ready, t.n + 1)
                        wait(eng, r_ready, t.n - 1)
                        eng.copy(xT[:, s, 1:1 + S].rearrange("c (p j) -> c j p", j=J),
                                 halves(T_BANK[s])).then_inc(xT_ready, 1)
                run_steps(eng, NB, LAG, step)

            def dve(eng):
                def step(t):
                    if t.within(NB):
                        wait(eng, t_ready, t.n - 1)
                        normalise(eng, xn[:, t.parity], t.n).then_inc(xn_ready, 1)
                    v = t.back(2)
                    if v.within(NB):
                        s = v.parity
                        eng.wait_ge(kv_ready, v.n + 1)
                        eng.wait_ge(gate_ready, v.n + 1)
                        wait(eng, updated, v.n - 1)
                        eng.tensor_tensor(branch[:, s, :, :], halves(KV_BANK[s]), gate[:, s, :, :],
                                          ALU.mult).then_inc(gated, 1)
                    k = t.back(1)
                    if k.within(NB):
                        s = k.parity
                        eng.wait_ge(relu_ready, k.n + 1)
                        wait(eng, kv_ready, k.n - 1)
                        eng.tensor_tensor(kact[:, s, :], relu[:, s, :], relu[:, s, :], ALU.mult).then_inc(kact_ready, 1)
                    if v.within(NB):
                        eng.wait_ge(gated, v.n + 1)
                        eng.tensor_tensor(seq(v.n), seq(v.n), branch[:, v.parity, :, :], ALU.add).then_inc(updated, 1)
                        eng.wait_ge(updated, v.n + 1)
                        add_stats(eng, v.n, done)
                run_steps(eng, NB, LAG, step)
                eng.wait_ge(done, J * NB)

            return pool, pe, act, dve

        work = sb("work", [P, 8 * 2 * S])

        def tile(at, shape):
            n = int(np.prod(shape))
            v = work[:, at * 2 * S:at * 2 * S + n]
            names = "abcd"[:len(shape)]
            sizes = {k: d for k, d in zip(names[1:], shape[1:])}
            return v.rearrange(f"p ({' '.join(names)}) -> p {' '.join(names)}", **sizes)

        relu, gate = tile(0, [2, S]), tile(1, [2, J, C])
        kact, branch = tile(2, [2, S]), tile(3, [2, J, C])

        qk = tile(0, [2, 2, S])
        vrow = tile(2, [2, J, C])
        nmax = sb("nmax", [P, 2, J])
        nmax_s = sb("nmax_s", [P, 2, J])
        den = sb("den", [P, 2, J])
        rden = sb("rden", [P, 2, J])
        prob = tile(3, [2, J, S])
        probT = tile(5, [2, J, S])
        orow = tile(7, [2, J, C])

        def attn0_layer(layer):
            names = ("xn_ready t_ready xT_ready qk_ready qk_copied v_ready v_copied s_ready max_ready bias_ready "
                     "exp_ready den_ready pT_ready pT_copied o_ready o_copied y_ready updated stats xb_ready").split()
            q = {n: sem(f"a{layer}_{n}") for n in names}
            LAG = 6
            T_BANK, QK_BANK, V_BANK, S_BANK, PT_BANK, O_BANK, Y_BANK = range(7)

            def pool(eng):
                eng.wait_ge(ln_ready, layer + 1)

                def step(t):
                    if t.within(NB):
                        eng.wait_ge(q["xn_ready"], t.n + 1)
                        eng.tensor_tensor(seq(t.n), seq(t.n), bproj_b[:, :, :], ALU.add).then_inc(q["xb_ready"], 1)
                run_steps(eng, NB, LAG, step)

            def pe(eng):
                def step(t):
                    y = t.back(4)
                    if y.within(NB):
                        eng.wait_ge(q["o_copied"], y.n + 1)
                        wait(eng, q["updated"], y.n)
                        for j in range(J):
                            mm = eng.matmul(halves(Y_BANK)[:, j, :], orow[:, y.parity, j, :], wT[:, WP, :],
                                            start=True, stop=True)
                        mm.then_inc(q["y_ready"], 1)
                    s_ = t.back(2)
                    if s_.within(NB):
                        s = s_.parity
                        eng.wait_ge(q["qk_copied"], s_.n + 1)
                        wait(eng, q["max_ready"], s_.n)
                        wait(eng, q["exp_ready"], J * s_.n)
                        for j in range(J):
                            mm = eng.matmul(halves(S_BANK, S)[:, j, :], qk[:, s, 0, j * P:(j + 1) * P], qk[:, s, 1, :],
                                            start=True, stop=True)
                        mm.then_inc(q["s_ready"], 1)
                    o = t.back(3)
                    if o.within(NB):
                        s = o.parity
                        eng.wait_ge(q["exp_ready"], J * (o.n + 1))
                        wait(eng, q["pT_copied"], o.n)
                        for c in range(J):
                            for j in range(J):
                                mm = eng.transpose(halves(PT_BANK, S)[:, c, j * P:(j + 1) * P],
                                                   prob[:, s, j, c * P:(c + 1) * P], ident[:, :])
                        mm.then_inc(q["pT_ready"], 1)
                    k = t.back(1)
                    if k.within(NB):
                        s = k.parity
                        eng.wait_ge(q["xT_ready"], k.n + 1)
                        wait(eng, q["qk_copied"], k.n)
                        for i, w in enumerate((WQ, WK)):
                            mm = eng.matmul(halves(QK_BANK, S)[:, i, :], wT[:, w, :], xT[:, s, 1:1 + S],
                                            start=True, stop=True)
                        mm.then_inc(q["qk_ready"], 1)
                        wait(eng, q["v_copied"], k.n)
                        for c in range(J):
                            mm = eng.matmul(halves(V_BANK)[:, c, :], xT[:, s, 1 + c * P:1 + (c + 1) * P], wT[:, WV, :],
                                            start=True, stop=True)
                        mm.then_inc(q["v_ready"], 1)
                    if t.within(NB):
                        eng.wait_ge(q["xn_ready"], t.n + 1)
                        wait(eng, q["xT_ready"], t.n)
                        for j in range(J):
                            mm = eng.transpose(halves(T_BANK)[:, j, :], xn[:, t.parity, j, :], ident[:, :])
                        mm.then_inc(q["t_ready"], 1)
                    if o.within(NB):
                        s = o.parity
                        eng.wait_ge(q["pT_copied"], o.n + 1)
                        eng.wait_ge(q["v_copied"], o.n + 1)
                        wait(eng, q["o_copied"], o.n)
                        for j in range(J):
                            for c in range(J):
                                mm = eng.matmul(halves(O_BANK)[:, j, :], probT[:, s, c, j * P:(j + 1) * P],
                                                vrow[:, s, c, :], start=(c == 0), stop=(c == J - 1))
                        mm.then_inc(q["o_ready"], 1)
                run_steps(eng, NB, LAG, step)

            def act(eng):
                layer_consts_act(eng, layer)

                def step(t):
                    if t.within(NB):
                        s = t.parity
                        eng.wait_ge(q["t_ready"], t.n + 1)
                        wait(eng, q["v_ready"], t.n - 1)
                        eng.copy(xT[:, s, 1:1 + S].rearrange("c (p j) -> c j p", j=J),
                                 halves(T_BANK)).then_inc(q["xT_ready"], 1)
                    s_ = t.back(2)
                    if s_.within(NB):
                        s = s_.parity
                        eng.wait_ge(q["bias_ready"], s_.n + 1)
                        wait(eng, q["pT_ready"], s_.n - 1)
                        for j in range(J):
                            eng.activation(prob[:, s, j, :], halves(S_BANK, S)[:, j, :], ACT.Exp,
                                           bias=nmax_s[:, s, j:j + 1], scale=ATTN0_SCALE,
                                           accum_out=den[:, s, j:j + 1]).then_inc(q["exp_ready"], 1)
                    k = t.back(1)
                    if k.within(NB):
                        s = k.parity
                        eng.wait_ge(q["qk_ready"], k.n + 1)
                        wait(eng, q["s_ready"], k.n - 1)
                        eng.copy(qk[:, s, :, :], halves(QK_BANK, S)).then_inc(q["qk_copied"], 1)
                        eng.wait_ge(q["v_ready"], k.n + 1)
                        wait(eng, q["o_ready"], k.n - 1)
                        eng.copy(vrow[:, s, :, :], halves(V_BANK)).then_inc(q["v_copied"], 1)
                run_steps(eng, NB, LAG, step)

            def dve(eng):
                def step(t):
                    if t.within(NB):
                        wait(eng, q["t_ready"], t.n - 1)
                        normalise(eng, xn[:, t.parity], t.n).then_inc(q["xn_ready"], 1)
                    y = t.back(4)
                    if y.within(NB):
                        eng.wait_ge(q["y_ready"], y.n + 1)
                        eng.wait_ge(q["xb_ready"], y.n + 1)
                        eng.tensor_tensor(seq(y.n), seq(y.n), halves(Y_BANK), ALU.add).then_inc(q["updated"], 1)
                    s_ = t.back(2)
                    if s_.within(NB):
                        s = s_.parity
                        eng.wait_ge(q["s_ready"], s_.n + 1)
                        eng.tensor_reduce(nmax[:, s, :], halves(S_BANK, S), AX_X, ALU.max,
                                          negate=True).then_inc(q["max_ready"], 1)
                        eng.wait_ge(q["max_ready"], s_.n + 1)
                        wait(eng, q["exp_ready"], J * (s_.n - 1))
                        eng.tensor_scalar(nmax_s[:, s, :], nmax[:, s, :], ATTN0_SCALE, None,
                                          ALU.mult).then_inc(q["bias_ready"], 1)
                    o = t.back(3)
                    if o.within(NB):
                        s = o.parity
                        eng.wait_ge(q["pT_ready"], o.n + 1)
                        wait(eng, q["o_ready"], o.n - 1)
                        eng.tensor_copy(probT[:, s, :, :], halves(PT_BANK, S)).then_inc(q["pT_copied"], 1)
                        eng.reciprocal(rden[:, s, :], den[:, s, :]).then_inc(q["den_ready"], 1)
                    if y.within(NB):
                        eng.wait_ge(q["updated"], y.n + 1)
                        add_stats(eng, y.n, q["stats"])
                    if o.within(NB):
                        s = o.parity
                        eng.wait_ge(q["den_ready"], o.n + 1)
                        eng.wait_ge(q["o_ready"], o.n + 1)
                        wait(eng, q["y_ready"], o.n - 1)
                        eng.tensor_tensor(orow[:, s, :, :], halves(O_BANK),
                                          rden[:, s, :].unsqueeze(2).to_broadcast([P, J, C]),
                                          ALU.mult).then_inc(q["o_copied"], 1)
                run_steps(eng, NB, LAG, step)
                eng.wait_ge(q["stats"], J * NB)

            return pool, pe, act, dve

        def tern_layer(layer, last):
            names = "xn_ready t_ready xT_ready y_ready updated stats xb_ready".split()
            q = {n: sem(f"t{layer}_{n}") for n in names}
            LAG = 4

            def pool(eng):
                eng.wait_ge(ln_ready, layer + 1)

                def step(t):
                    if t.within(NB):
                        eng.wait_ge(q["xn_ready"], t.n + 1)
                        eng.tensor_tensor(seq(t.n), seq(t.n), btern_b[:, :, :], ALU.add).then_inc(q["xb_ready"], 1)
                run_steps(eng, NB, LAG, step)

            def pe(eng):
                def step(t):
                    k = t.back(1)
                    if k.within(NB):
                        s = k.parity
                        eng.wait_ge(q["xT_ready"], k.n + 1)
                        wait(eng, q["updated"], k.n - 1)
                        for j in range(J):
                            mm = eng.matmul(halves(2 + s)[:, j, :], xT[:, s, 1 + j * P:1 + (j + 1) * P], wT[:, TW, :],
                                            start=True, stop=True)
                        mm.then_inc(q["y_ready"], 1)
                    if t.within(NB):
                        eng.wait_ge(q["xn_ready"], t.n + 1)
                        wait(eng, q["xT_ready"], t.n - 1)
                        for j in range(J):
                            mm = eng.transpose(halves(t.parity)[:, j, :], xn[:, t.parity, j, :], ident[:, :])
                        mm.then_inc(q["t_ready"], 1)
                run_steps(eng, NB, LAG, step)

            def act(eng):
                layer_consts_act(eng, layer)

                def step(t):
                    if t.within(NB):
                        eng.wait_ge(q["t_ready"], t.n + 1)
                        wait(eng, q["y_ready"], t.n - 1)
                        eng.copy(xT[:, t.parity, 1:1 + S], banks[t.parity][:, 0:S]).then_inc(q["xT_ready"], 1)
                run_steps(eng, NB, LAG, step)

            def dve(eng):
                def step(t):
                    k = t.back(1)
                    if t.within(NB):
                        wait(eng, q["t_ready"], t.n - 1)
                        normalise(eng, xn[:, t.parity], t.n).then_inc(q["xn_ready"], 1)
                    if k.within(NB):
                        eng.wait_ge(q["y_ready"], k.n + 1)
                        eng.wait_ge(q["xb_ready"], k.n + 1)
                        eng.tensor_tensor(seq(k.n), seq(k.n), halves(2 + k.parity), ALU.add).then_inc(q["updated"], 1)
                    if not last:
                        d = t.back(2)
                        if d.within(NB):
                            eng.wait_ge(q["updated"], d.n + 1)
                            add_stats(eng, d.n, q["stats"])
                run_steps(eng, NB, LAG, step)
                if not last:
                    eng.wait_ge(q["stats"], J * NB)

            def sync(eng):
                if last:
                    for b in range(0, NB, LOAD):
                        eng.wait_ge(q["updated"], b + LOAD)
                        eng.dma_start(xout_v[:, b:b + LOAD, :], x_flat[:, b:b + LOAD, :]).then_inc(stored, 16)
                    eng.wait_ge(stored, 16 * (NB // LOAD))

            return pool, pe, act, dve, sync

        wqk_hi = sb("wqk_hi", [P, 2, H * D], F32R)
        wqk_lo = sb("wqk_lo", [P, 2, H * D], F32R)
        wv_hi = sb("wv_hi", [P, H * D], F32R)
        wv_lo = sb("wv_lo", [P, H * D], F32R)
        w1_raw = sb("w1_raw", [P, 512])
        wout = sb("wout", [P, PAIRS, C])
        bqk = sb("bqk", [P, 2, PAIRS])
        bv_b = sb("bv_b", [P, H * D])
        pos = sb("pos", [P, S])
        x_hi = sb("x_hi", [P, 2, S], F32R)
        x_lo = sb("x_lo", [P, 2, S], F32R)
        qk_parts = sb("qk_parts", [P, 2, 4, PAIRS, S], F32R)
        q_twice = qk_parts[:, :, 0, :, :]
        q_rest = qk_parts[:, :, 3, :, :]
        k_ones = qk_parts[:, :, 1, :, :]
        k_parts = qk_parts[:, :, 2, :, :]
        k_sum = sb("k_sum", [P, 2, S])
        v1 = sb("v1", [P, J, H, VW])
        nm1 = sb("nm1", [P, 2, 2 * J])
        m_rows = sb("m_rows", [2 * J, 2, P], F32R)
        p1 = sb("p1", [P, 2, 2, J, S])
        rden1 = sb("rden1", [P, 2, 2, J])
        o1 = tile(0, [J, H, D])
        o1T = tile(4, [PAIRS, S])

        w1_loaded = sem("w1_loaded")
        w1_slice = sem("w1_slice_loaded")
        w1_split = sem("w1_split")
        attn1_ready = sem("attn1_consts_ready")
        bqk_scaled = sem("bqk_scaled")

        def attn1_setup_sync(sp):
            sp.dma_start(wout[:, :, :], W_out1.rearrange("(i p) e -> p i e", p=P)).then_inc(w1_loaded, 16)
            sp.dma_start(pos[0:D, :], pos_t).then_inc(w1_loaded, 16)
            sp.dma_start(pos[D:P, :], pos_t).then_inc(w1_loaded, 16)
            for i in range(2):
                for pr in range(PAIRS):
                    at = i * H * D + pr * P
                    sp.dma_start(bqk[:, i, pr:pr + 1],
                                 b_qkv1[at:at + P].rearrange("(c o) -> c o", o=1)).then_inc(w1_loaded, 16)
            sp.dma_start(bv_b[:, :], b_qkv1[2 * H * D:3 * H * D].rearrange("(o c) -> o c", o=1)
                         .to_broadcast([P, H * D])).then_inc(w1_loaded, 16)
            for k in range(6):
                wait(sp, w1_split, 2 * k)
                sp.dma_start(w1_raw[:, :], W_qkv1[:, k * 512:(k + 1) * 512]).then_inc(w1_slice, 16)

        def attn1_setup_dve(dve):
            dve.wait_ge(w1_loaded, 16 * (3 + 2 * PAIRS + 1))
            dve.tensor_scalar(bqk[:, 0, :], bqk[:, 0, :], 0.125, None, ALU.mult).then_inc(bqk_scaled, 1)
            for k in range(6):
                dve.wait_ge(w1_slice, 16 * (k + 1))
                part = slice((k % 2) * 512, (k % 2 + 1) * 512)
                hi, lo = ((wqk_hi[:, k // 2, part], wqk_lo[:, k // 2, part]) if k < 4
                          else (wv_hi[:, part], wv_lo[:, part]))
                f = 0.125 if k < 2 else 1.0
                dve.tensor_scalar(hi, w1_raw[:, :], f, None, ALU.mult).then_inc(w1_split, 1)
                dve.wait_ge(w1_split, 2 * k + 1)
                dve.scalar_tensor_tensor(out=lo, in0=w1_raw[:, :], scalar=f, in1=hi.bitcast(F32),
                                         op0=ALU.mult, op1=ALU.subtract).then_inc(w1_split, 1)
            dve.wait_ge(w1_split, 12)

        def attn1_setup_pool(pool):
            for tile in (q_rest, k_ones):
                pool.memset(tile[:, :, :, :].bitcast(F32), 0.0).then_inc(attn1_ready, 1)
            pool.memset(v1[:, :, :, D:VW], 1.0).then_inc(attn1_ready, 1)
            pool.wait_ge(attn1_ready, 3)
            pool.memset(k_ones[D:D + 1, 0, :, :].bitcast(F32), 1.0).then_inc(attn1_ready, 1)
            pool.wait_ge(attn1_ready, 4)
            pool.memset(k_ones[0:1, 1, :, :].bitcast(F32), 1.0).then_inc(attn1_ready, 1)
            pool.wait_ge(attn1_ready, N_ATTN1_READY)
        N_ATTN1_READY = 2 + 1 + 2

        class Pair:

            def __init__(self, b, odd, pr):
                self.b, self.odd, self.pr = b, odd, pr
                self.n = b * PAIRS + pr
                self.slot = pr % 2

            def back(self, lag):
                seqs = (lag - self.pr + PAIRS - 1) // PAIRS if lag > self.pr else 0
                return Pair(self.b - seqs, (self.odd + seqs) % 2, (self.pr - lag) % PAIRS)

            @property
            def exists(self):
                return not isinstance(self.b, int) or 0 <= self.b < NB

        def run_pairs(eng, step):
            for b in (0, 1):
                for pr in range(PAIRS):
                    step(Pair(b, b, pr))
            with eng.Fori(1, NB // 2 - 1) as half:
                for odd in (0, 1):
                    for pr in range(PAIRS):
                        step(Pair(half * 2 + odd, odd, pr))
            for b in (NB - 2, NB - 1, NB):
                for pr in range(PAIRS):
                    step(Pair(b, b % 2, pr))

        MISC_USES = [(0, 1, "turn", 0, 1), (1, 0, "turn", 1, 1), (1, 1, "values", 0, 0), (2, 0, "values", 1, 0),
                     (3, 0, "turn", 2, 1), (4, 0, "tokens", 0, -1), (5, 0, "turn", 3, 1), (5, 1, "values", 2, 0),
                     (6, 0, "values", 3, 0), (6, 1, "output", 0, 1), (7, 0, "output", 1, 1), (7, 1, "output", 2, 1)]
        OUT_LAST = 2

        def misc_use(t, place):
            for pr, at, what, part, back in MISC_USES:
                if (pr, at) == (t.pr, place):
                    b = t.b - back
                    if not isinstance(b, int) or 0 <= b < NB:
                        return what, part, b
            return None

        def misc_before(t, place):
            k = [u[:2] for u in MISC_USES].index((t.pr, place))
            b = t.b
            while True:
                k -= 1
                if k < 0:
                    k, b = len(MISC_USES) - 1, b - 1
                if isinstance(b, int) and b < 0:
                    return "tokens", 0, 0
                _, _, what, part, back = MISC_USES[k]
                if not isinstance(b, int) or 0 <= b - back < NB:
                    return what, part, b - back

        def attn1_layer(layer):
            names = ("xn_ready t_ready x_hi_ready x_lo_ready k_ready q_ready q_hi_ready "
                     "q_lo_ready k_sum_ready k_hi_ready k_lo_ready v_ready v_copied max_scored max_ready mT_ready "
                     "mT_copied m_placed scores_ready exp_ready pv_ready rden_ready o_copied oT_ready oT_copied "
                     "y_ready updated stats xb_ready").split()
            q = {n: sem(f"b_{n}") for n in names}
            again_placed = [sem(f"b_again_placed{i}") for i in range(4)]
            Q_BANK, K_BANK, MAX_BANK, MISC, S_BANK, O_BANK = 0, 1, 2, 3, (4, 5), (6, 7)
            HALF = (slice(0, D), slice(D, P))
            VG = J * G
            TG = PAIRS // 2
            SPLIT_Q, MAXIMA, SCORES, WEIGH_ODD = 1, 3, 4, 5

            def o_pair(slot):
                return banks[O_BANK[slot]][:, 0:2 * J * VW].rearrange("p (h j w) -> p h j w", h=2, j=J)

            def pe(eng):
                def scores(u, par):
                    if par == 0:
                        eng.wait_ge(q["m_placed"], 32 * (u.n + 1))
                        eng.wait_ge(q["q_lo_ready"], 2 * (u.n + 1))
                    wait(eng, q["exp_ready"], 2 * u.n + par - 1)
                    for c in range(J):
                        keys = slice(c * P, (c + 1) * P)
                        out = halves(S_BANK[par], S)[:, c, :]
                        eng.matmul(out, k_parts[:, par, u.pr, keys], q_twice[:, par, u.pr, :], start=True, stop=False)
                        mm = eng.matmul(out, k_ones[:, par, u.pr, keys], q_rest[:, par, u.pr, :],
                                        start=False, stop=True)
                    mm.then_inc(q["scores_ready"], 1)

                def project(u, z):
                    if z == 1 and u.pr == 0:
                        eng.wait_ge(q["x_lo_ready"], u.b + 1)
                    wait(eng, q["k_sum_ready"] if z else q["q_lo_ready"], u.n if z else 2 * u.n)
                    cols = slice(u.pr * P, (u.pr + 1) * P)
                    out = banks[K_BANK if z else Q_BANK][:, 0:S]
                    eng.matmul(out, wqk_hi[:, z, cols], x_hi[:, u.odd, :], start=True, stop=False)
                    eng.matmul(out, wqk_hi[:, z, cols], x_lo[:, u.odd, :], start=False, stop=False)
                    eng.matmul(out, wqk_lo[:, z, cols], x_hi[:, u.odd, :], start=False,
                               stop=True).then_inc(q["k_ready"] if z else q["q_ready"], 1)

                def row_max(u, par):
                    if par == 0:
                        eng.wait_ge(again_placed[u.pr % 4], 32 * (2 * u.b + u.pr // 4 + 1))
                        eng.wait_ge(q["k_lo_ready"], 2 * (u.n + 1))
                        wait(eng, q["mT_copied"], u.n)
                    else:
                        eng.wait_ge(q["max_ready"], 2 * u.n + 1)
                    for j in range(J):
                        mm = eng.matmul(halves(MAX_BANK, S)[:, j, :], q_twice[:, par, u.pr, j * P:(j + 1) * P],
                                        k_parts[:, par, u.pr, :], start=True, stop=True)
                    mm.then_inc(q["max_scored"], 1)

                def turn_maxima(u):
                    eng.wait_ge(q["max_ready"], 2 * (u.n + 1))
                    eng.transpose(banks[MAX_BANK][0:2 * J, 0:P], nm1[:, u.slot, :],
                                  ident[:, :]).then_inc(q["mT_ready"], 1)

                def weigh(u, par):
                    eng.wait_ge(q["exp_ready"], 2 * u.n + par + 1)
                    if par == 0:
                        if u.pr % PG == 0:
                            eng.wait_ge(q["v_copied"], u.b * VG + J * (u.pr // PG + 1))
                        wait(eng, q["o_copied"], u.n - 1)
                    for j in range(J):
                        for c in range(J):
                            mm = eng.matmul(o_pair(u.slot)[:, par, j, :], p1[:, u.slot, par, c, j * P:(j + 1) * P],
                                            v1[:, c, 2 * u.pr + par, :], start=(c == 0), stop=(c == J - 1))
                    mm.then_inc(q["pv_ready"], 1)

                def misc(t, place):
                    use = misc_use(t, place)
                    if use is None:
                        return
                    what, part, b = use
                    last, last_part, last_b = misc_before(t, place)
                    if last == "values":
                        eng.wait_ge(q["v_copied"], last_b * VG + last_part + 1)
                    elif last == "turn":
                        eng.wait_ge(q["oT_copied"], last_b * TG + last_part + 1)
                    elif last == "tokens":
                        eng.wait_ge(q["x_lo_ready"], last_b + 1)
                    elif last_part == OUT_LAST:
                        eng.wait_ge(q["updated"], last_b + 1)
                    if what == "values":
                        g, j = part // J, part % J
                        cols = slice(g * HG * D, (g + 1) * HG * D)
                        toks = slice(j * P, (j + 1) * P)
                        out = banks[MISC][:, :]
                        hi, lo = x_hi[:, t.odd, toks], x_lo[:, t.odd, toks]
                        eng.matmul(out, hi, wv_hi[:, cols], start=True, stop=False)
                        eng.matmul(out, hi, wv_lo[:, cols], start=False, stop=False)
                        eng.matmul(out, lo, wv_hi[:, cols], start=False, stop=True).then_inc(q["v_ready"], 1)
                    elif what == "turn":
                        eng.wait_ge(q["o_copied"], b * PAIRS + 2 * (part + 1))
                        for i in range(2):
                            for j in range(J):
                                mm = eng.transpose(banks[MISC][:, (i * J + j) * P:(i * J + j + 1) * P],
                                                   o1[:, j, 4 * part + 2 * i:4 * part + 2 * i + 2, :]
                                                   .rearrange("p h d -> p (h d)"), ident[:, :])
                        mm.then_inc(q["oT_ready"], 1)
                    elif what == "output":
                        if part == 0:
                            eng.wait_ge(q["oT_copied"], TG * (b + 1))
                        j, pairs = ((0, (0, 1, 2, 3)), (0, (4, 5, 6, 7)), (1, range(PAIRS)))[part]
                        for i in pairs:
                            mm = eng.matmul(halves(MISC)[:, j, :], o1T[:, i, j * P:(j + 1) * P],
                                            wout[:, i, :], start=(i == 0), stop=(i == PAIRS - 1))
                        if part == OUT_LAST:
                            mm.then_inc(q["y_ready"], 1)
                    else:
                        turn_tokens(b)

                def turn_tokens(b):
                    eng.wait_ge(q["xn_ready"], b + 1)
                    for j in range(J):
                        mm = eng.transpose(halves(MISC)[:, j, :], xn[:, 0, j, :], ident[:, :])
                    mm.then_inc(q["t_ready"], 1)

                def step(t):
                    m, b, w = t.back(MAXIMA), t.back(SCORES), t.back(WEIGH_ODD)
                    if m.exists:
                        row_max(m, 0)
                    if t.exists:
                        project(t, 1)
                    if w.exists:
                        weigh(w, 1)
                    if m.exists:
                        row_max(m, 1)
                    misc(t, 0)
                    if b.exists:
                        scores(b, 0)
                        scores(b, 1)
                    if m.exists:
                        turn_maxima(m)
                    if t.exists:
                        project(t, 0)
                    misc(t, 1)
                    if b.exists:
                        weigh(b, 0)

                turn_tokens(0)
                run_pairs(eng, step)

            def act(eng):
                layer_consts_act(eng, layer)
                eng.wait_ge(attn1_ready, N_ATTN1_READY)
                eng.wait_ge(bqk_scaled, 1)

                def exp(u, par):
                    eng.wait_ge(q["scores_ready"], 2 * u.n + par + 1)
                    wait(eng, q["pv_ready"], 2 * (u.n - 2) + par + 1)
                    eng.activation(p1[:, u.slot, par, :, :], halves(S_BANK[par], S), ACT.Exp).then_inc(q["exp_ready"], 1)

                def token_hi(b, odd):
                    eng.wait_ge(q["t_ready"], b + 1)
                    eng.copy(x_hi[:, odd, :], banks[MISC][:, 0:S]).then_inc(q["x_hi_ready"], 1)

                def misc(t, place):
                    use = misc_use(t, place)
                    if use is None:
                        return
                    what, part, b = use
                    if what == "turn":
                        eng.wait_ge(q["oT_ready"], b * TG + part + 1)
                        wait(eng, q["y_ready"], b)
                        eng.copy(o1T[:, 2 * part:2 * part + 2, :], halves(MISC, S)).then_inc(q["oT_copied"], 1)
                    elif what == "tokens":
                        token_hi(b, 1 - t.odd)

                def step(t):
                    b = t.back(SCORES)
                    misc(t, 0)
                    if b.exists:
                        exp(b, 0)
                        exp(b, 1)
                    misc(t, 1)
                    if t.exists:
                        eng.wait_ge(q["k_sum_ready"], t.n + 1)
                        for par in range(2):
                            r = HALF[par]
                            eng.copy(k_ones[r, par, t.pr, :], k_sum[r, t.slot, :]).then_inc(q["k_hi_ready"], 1)
                        eng.wait_ge(q["q_ready"], t.n + 1)
                        for par in range(2):
                            r = HALF[par]
                            eng.activation(q_twice[r, par, t.pr, :], banks[Q_BANK][r, 0:S], ACT.Identity,
                                           bias=bqk[r, 0, t.pr:t.pr + 1]).then_inc(q["q_hi_ready"], 1)

                token_hi(0, 0)
                run_pairs(eng, step)

            def dve(eng):
                eng.wait_ge(attn1_ready, N_ATTN1_READY)
                eng.wait_ge(bqk_scaled, 1)

                def norm(u):
                    eng.wait_ge(q["pv_ready"], 2 * (u.n + 1))
                    wait(eng, q["o_copied"], u.n - 1)
                    eng.reciprocal(rden1[:, u.slot, :, :], o_pair(u.slot)[:, :, :, D]).then_inc(q["rden_ready"], 1)
                    eng.wait_ge(q["rden_ready"], u.n + 1)
                    wait(eng, q["oT_ready"], (u.b - 1) * TG + u.pr // 2 + 1)
                    eng.tensor_tensor(o1[:, :, 2 * u.pr:2 * u.pr + 2, :].rearrange("p j h d -> p h j d"),
                                      o_pair(u.slot)[:, :, :, 0:D],
                                      rden1[:, u.slot, :, :].unsqueeze(3).to_broadcast([P, 2, J, D]),
                                      ALU.mult).then_inc(q["o_copied"], 1)

                def reduce(u, par):
                    eng.wait_ge(q["max_scored"], 2 * u.n + par + 1)
                    wait(eng, q["mT_ready"], u.n - 1)
                    eng.tensor_reduce(nm1[:, u.slot, par * J:(par + 1) * J], halves(MAX_BANK, S), AX_X, ALU.max,
                                      negate=True).then_inc(q["max_ready"], 1)

                def token_lo(b, odd):
                    eng.wait_ge(q["x_hi_ready"], b + 1)
                    eng.tensor_tensor(x_lo[:, odd, :], banks[MISC][:, 0:S], x_hi[:, odd, :].bitcast(F32),
                                      ALU.subtract).then_inc(q["x_lo_ready"], 1)

                def misc(t, place):
                    use = misc_use(t, place)
                    if use is None:
                        return
                    what, part, b = use
                    if what == "values":
                        g, j = part // J, part % J
                        cols = slice(g * HG * D, (g + 1) * HG * D)
                        eng.wait_ge(q["v_ready"], b * VG + part + 1)
                        wait(eng, q["pv_ready"], (b - 1) * H + (g + 1) * HG)
                        eng.tensor_tensor(v1[:, j, g * HG:(g + 1) * HG, 0:D],
                                          banks[MISC][:, :].rearrange("p (h d) -> p h d", d=D),
                                          bv_b[:, cols].rearrange("p (h d) -> p h d", d=D),
                                          ALU.add).then_inc(q["v_copied"], 1)
                    elif what == "output" and part == OUT_LAST:
                        eng.wait_ge(q["y_ready"], b + 1)
                        eng.wait_ge(q["xb_ready"], b + 1)
                        eng.tensor_tensor(seq(b), seq(b), halves(MISC), ALU.add).then_inc(q["updated"], 1)
                        eng.wait_ge(q["updated"], b + 1)
                        add_stats(eng, b, q["stats"])
                    elif what == "tokens":
                        token_lo(b, 1 - t.odd)

                def step(t):
                    h, m, w = t.back(SPLIT_Q), t.back(MAXIMA), t.back(WEIGH_ODD)
                    if t.pr == 3 and (not isinstance(t.b, int) or t.b < NB - 1):
                        eng.wait_ge(q["t_ready"], t.b + 1)
                        normalise(eng, xn[:, 0], t.b + 1).then_inc(q["xn_ready"], 1)
                    if m.exists:
                        reduce(m, 0)
                    if h.exists:
                        for par in range(2):
                            r = HALF[par]
                            eng.wait_ge(q["q_hi_ready"], 2 * h.n + par + 1)
                            eng.scalar_tensor_tensor(out=q_rest[r, par, h.pr, :], in0=banks[Q_BANK][r, 0:S],
                                                     scalar=bqk[r, 0, h.pr:h.pr + 1],
                                                     in1=q_twice[r, par, h.pr, :].bitcast(F32),
                                                     op0=ALU.add, op1=ALU.subtract).then_inc(q["q_lo_ready"], 1)
                    if m.exists:
                        reduce(m, 1)
                    misc(t, 0)
                    if m.exists:
                        eng.wait_ge(q["mT_ready"], m.n + 1)
                        wait(eng, q["m_placed"], 32 * (m.n - 1))
                        eng.tensor_copy(m_rows[:, m.slot, :], banks[MAX_BANK][0:2 * J, 0:P]).then_inc(q["mT_copied"], 1)
                    if t.exists:
                        eng.wait_ge(q["k_ready"], t.n + 1)
                        wait(eng, q["k_lo_ready"], 2 * (t.n - 1))
                        wait(eng, q["k_hi_ready"], 2 * (t.n - 1))
                        eng.scalar_tensor_tensor(out=k_sum[:, t.slot, :], in0=banks[K_BANK][:, 0:S],
                                                 scalar=bqk[:, 1, t.pr:t.pr + 1], in1=pos[:, :], op0=ALU.add,
                                                 op1=ALU.add).then_inc(q["k_sum_ready"], 1)
                    if w.exists:
                        norm(w)
                    misc(t, 1)

                normalise(eng, xn[:, 0], 0).then_inc(q["xn_ready"], 1)
                token_lo(0, 0)
                run_pairs(eng, step)
                eng.wait_ge(q["stats"], J * NB)

            def pool(eng):
                eng.wait_ge(ln_ready, layer + 1)

                def step(t):
                    if not t.exists:
                        return
                    for par in range(2):
                        r = HALF[par]
                        eng.wait_ge(q["k_hi_ready"], 2 * t.n + par + 1)
                        wait(eng, q["k_lo_ready"], 2 * t.n + par)
                        eng.tensor_tensor(k_parts[r, par, t.pr, :], k_sum[r, t.slot, :],
                                          k_ones[r, par, t.pr, :].bitcast(F32), ALU.subtract).then_inc(q["k_lo_ready"], 1)
                    if t.pr == 2:
                        eng.wait_ge(q["k_lo_ready"], 2 * (t.n + 1))
                        eng.wait_ge(q["xn_ready"], t.b + 1)
                        eng.tensor_tensor(seq(t.b), seq(t.b), bout_b[:, :, :], ALU.add).then_inc(q["xb_ready"], 1)
                run_pairs(eng, step)

            def sync(eng):
                def step(t):
                    h, m = t.back(SPLIT_Q), t.back(MAXIMA)
                    if h.exists:
                        for par in range(2):
                            r, o = HALF[par], HALF[1 - par]
                            eng.wait_ge(q["q_hi_ready"], 2 * h.n + par + 1)
                            eng.wait_ge(q["k_hi_ready"], 2 * h.n + par + 1)
                            eng.dma_start(qk_parts[o, par, 0:3:2, h.pr, :].bitcast(F32),
                                          qk_parts[r, par, 0:2, h.pr, :].bitcast(F32)
                                          ).then_inc(again_placed[h.pr % 4], 16)
                    if m.exists:
                        eng.wait_ge(q["mT_copied"], m.n + 1)
                        for par, row in ((0, D), (1, 0)):
                            eng.dma_start(q_rest[row:row + 1, par, m.pr, :].bitcast(F32)
                                          .rearrange("o (j p) -> o j p", j=J),
                                          m_rows[par * J:(par + 1) * J, m.slot, :].bitcast(F32)
                                          ).then_inc(q["m_placed"], 16)
                run_pairs(eng, step)

            return pool, pe, act, dve, sync

        ffn_a = ffn_layer(0)
        attn_b = attn0_layer(1)
        ffn_c = ffn_layer(2)
        tern_d = tern_layer(3, last=False)
        attn_e = attn1_layer(4)
        tern_f = tern_layer(5, last=True)
        layers = (ffn_a, attn_b, ffn_c, tern_d, attn_e, tern_f)

        block = ctx.enter_context(nc.Block())

        @block.sync
        def _(sp):
            setup_sync(sp)
            attn1_setup_sync(sp)
            attn_e[4](sp)
            tern_f[4](sp)

        @block.gpsimd
        def _(pool):
            setup_pool(pool)
            attn1_setup_pool(pool)
            for layer in layers:
                layer[0](pool)

        @block.tensor
        def _(pe):
            setup_pe(pe)
            for layer in layers:
                layer[1](pe)

        @block.scalar
        def _(act):
            for layer in layers:
                layer[2](act)

        @block.vector
        def _(dve):
            setup_dve(dve)
            for layer in layers:
                if layer is attn_e:
                    attn1_setup_dve(dve)
                layer_consts_dve(dve)
                layer[3](dve)


_INS = ['L0_attn_x', 'L0_attn_w_qkv', 'L0_attn_w_proj', 'L0_attn_b_proj', 'L0_ffn_W_r', 'L0_ffn_W_k', 'L0_ffn_W_v',
        'L0_ffn_mu_r', 'L0_ffn_mu_k', 'L1_attn_W_qkv', 'L1_attn_b_qkv', 'L1_attn_W_out', 'L1_attn_b_out',
        'L1_ffn_weight', 'L1_ffn_alpha', 'L1_ffn_bias']


def position_table():
    positions = np.arange(S, dtype=np.float32)[:, None]
    div = np.exp(np.arange(0, D, 2, dtype=np.float32) * np.float32(-(np.log(10000.0) / D)))
    table = np.zeros((S, D), np.float32)
    table[:, 0::2] = np.sin(positions * div)
    table[:, 1::2] = np.cos(positions * div)
    return np.ascontiguousarray(table.reshape(P, J, D).transpose(2, 1, 0).reshape(D, S))


def kernel(**inputs):
    import concourse.bacc as _bacc
    from concourse.bass_utils import run_bass_kernel_spmd as _run

    nc = _bacc.Bacc("TRN2", target_bir_lowering=False, num_devices=1)
    arrays, args = {}, []
    for name in _INS:
        a = np.ascontiguousarray(inputs[name])
        arrays[f"in_{name}"] = a
        args.append(nc.dram_tensor(f"in_{name}", a.shape, mybir.dt.from_np(a.dtype), kind="ExternalInput").ap())
    arrays["position_table"] = position_table()
    args.append(nc.dram_tensor("position_table", (D, S), F32, kind="ExternalInput").ap())
    args.append(nc.dram_tensor("out", (NB, S, C), F32, kind="ExternalOutput").ap())
    macaron_kernel(nc, *args)
    r = _run(nc, [arrays], core_ids=[0])
    return r.results[0]["out"]
```

```python
from contextlib import ExitStack

import numpy as np

import concourse.bass as bass
from concourse import mybir

F32 = mybir.dt.float32
F32R = mybir.dt.float32r
ALU = mybir.AluOpType
ACT = mybir.ActivationFunctionType
AX_X = mybir.AxisListType.X

P = 128
NB, S, C = 32, 256, 128
J = S // P
H, D = 16, 64
PAIRS = H // 2
G = 2
HG = H // G
PG = PAIRS // G
VW = 96
ATTN0_SCALE = float(1.0 / np.sqrt(8.0).astype(np.float32))
EPS = 1e-5
LOAD = 4
UNROLL = 8


class Step:

    def __init__(self, turn, at):
        self.turn, self.at = turn, at
        self.parity = at % 2

    def back(self, lag):
        return Step(self.turn, self.at - lag)

    @property
    def n(self):
        return self.turn * UNROLL + self.at

    def within(self, count):
        return not isinstance(self.turn, int) or 0 <= self.n < count


def run_steps(eng, count, lag, step):
    for t in range(lag):
        step(Step(0, t))
    with eng.Fori(lag // UNROLL, count // UNROLL) as turn:
        for at in range(UNROLL):
            step(Step(turn, at))
    for t in range(count, count + lag):
        step(Step(0, t))


def wait(eng, sem, value):
    if isinstance(value, int) and value <= 0:
        return
    eng.wait_ge(sem, value)


def macaron_kernel(nc, x_in, w_qkv0, w_proj0, b_proj0, W_r, W_k, W_v, mu_r, mu_k,
                   W_qkv1, b_qkv1, W_out1, b_out1, w_tern, alpha, bias_tern, pos_t, x_out):
    ctx = ExitStack()
    with ctx:
        def sb(name, shape, dt=F32):
            return ctx.enter_context(nc.sbuf_tensor(name, shape, dt))

        def sem(name):
            return ctx.enter_context(nc.semaphore(name))

        x = sb("x", [P, NB, J, C])
        ident = sb("ident", [P, P])
        ones = sb("ones", [P, P])
        stats = sb("stats", [P, NB * J, 6])
        rstd = sb("rstd", [P, NB * J])
        nbias = sb("nbias", [P, NB * J])
        lnt = sb("lnt", [P, 3, NB * J])
        warm = sb("warm", [P, 6])

        w_raw = sb("w_raw", [P, 8, P])
        wT = sb("wT", [P, 8, P])
        WQ, WK, WV, WP, FR, FK, FV, TW = range(8)
        wr_now, wr_prev = sb("wr_now", [P, P]), sb("wr_prev", [P, P])
        mu = sb("mu", [P, 4])
        bproj_b = sb("bproj_b", [P, J, C])
        bout_b = sb("bout_b", [P, J, C])
        btern_b = sb("btern_b", [P, J, C])
        alpha_b = sb("alpha_b", [P, 1])
        tern = sb("tern", [P, 4])
        ternm = sb("ternm", [P, P])

        xn = sb("xn", [P, 2, J, C])
        xT = sb("xT", [P, 2, 1 + S])

        xk_prev = sb("xk_prev", [P, 2, 1 + S])

        banks = [ctx.enter_context(nc.psum_tensor(f"bank{i}", [P, 512], F32)) for i in range(8)]

        def halves(b, w=C):
            return banks[b][:, 0:J * w].rearrange("p (j c) -> p j c", j=J)

        consts_ready = sem("consts_ready")
        loaded = [sem(f"x_loaded{i}") for i in range(NB // LOAD)]
        stored = sem("x_stored")
        w_loaded = sem("w_loaded")
        bias_loaded = sem("bias_loaded")
        ident_zeroed = sem("ident_zeroed")
        wT_ready = sem("wT_ready")
        w_ready = sem("w_ready")
        chain = sem("dve_chain")
        ln_var = sem("ln_var")
        ln_std = sem("ln_std")
        ln_ready = sem("ln_ready")
        tern_sum = sem("tern_sum")

        xin_v = x_in.rearrange("b (p j) c -> p b (j c)", j=J)
        xout_v = x_out.rearrange("b (p j) c -> p b (j c)", j=J)
        x_flat = x[:, :, :, :].rearrange("p b j c -> p b (j c)")
        x_chunks = x[:, :, :, :].rearrange("p b j c -> p (b j) c")

        chain_count = [0]

        def chained(dve, ins):
            chain_count[0] += 1
            ins.then_inc(chain, 1)
            dve.wait_ge(chain, chain_count[0])

        def setup_sync(sp):
            def load_x(b):
                sp.dma_start(x_flat[:, b:b + LOAD, :], xin_v[:, b:b + LOAD, :]).then_inc(loaded[b // LOAD], 16)

            for b in range(0, NB // 2, LOAD):
                load_x(b)
            sp.dma_start(w_raw[:, WQ:WV + 1, :], w_qkv0.rearrange("(k p) c -> p k c", p=P)).then_inc(w_loaded, 16)
            for k, w in ((WP, w_proj0), (FR, W_r), (FK, W_k), (FV, W_v), (TW, w_tern)):
                sp.dma_start(w_raw[:, k, :], w).then_inc(w_loaded, 16)
            sp.dma_start(mu[:, 0:1], mu_r.rearrange("(c o) -> c o", o=1)).then_inc(w_loaded, 16)
            sp.dma_start(mu[:, 1:2], mu_k.rearrange("(c o) -> c o", o=1)).then_inc(w_loaded, 16)
            sp.dma_start(alpha_b[:, :], alpha.rearrange("(o c) -> o c", o=1).to_broadcast([P, 1])).then_inc(w_loaded, 16)
            for b in range(NB // 2, NB, LOAD):
                load_x(b)
            for tile, b in ((bproj_b, b_proj0), (bout_b, b_out1), (btern_b, bias_tern)):
                row = b.rearrange("(o c) -> o c", o=1).to_broadcast([P, C])
                for j in range(J):
                    sp.dma_start(tile[:, j, :], row).then_inc(bias_loaded, 16)

        N_WDMA = 1 + 5 + 2 + 1
        N_BDMA = 3 * J

        def setup_pool(pool):
            pool.memset(ident[:, :], 0.0).then_inc(ident_zeroed, 1)
            pool.wait_ge(ident_zeroed, 1)
            pool.affine_select(out=ident[:, :], in_=ident[:, :], compare_op=ALU.not_equal, fill=1.0, base=0,
                               pattern=[[-1, P]], channel_multiplier=1).then_inc(consts_ready, 1)
            pool.memset(xT[:, :, 0:1], 0.0).then_inc(consts_ready, 1)
            pool.memset(xk_prev[:, :, 0:1], 0.0).then_inc(consts_ready, 1)
            pool.memset(ones[:, :], 1.0).then_inc(consts_ready, 1)

        def setup_pe(pe):
            pe.wait_ge(w_loaded, 16 * N_WDMA)
            pe.wait_ge(consts_ready, 4)
            for k in range(8):
                mm = pe.transpose(banks[k // 4][:, (k % 4) * P:(k % 4 + 1) * P], w_raw[:, k, :], ident[:, :])
            mm.then_inc(wT_ready, 1)
            pe.wait_ge(tern_sum, 1)
            pe.matmul(banks[2][:, 0:1], ones[:, :], tern[:, 0:1], start=True, stop=True).then_inc(tern_sum, 1)

        def setup_dve(dve):
            def stats_of(seqs):
                for b in seqs:
                    if b % LOAD == 0:
                        dve.wait_ge(loaded[b // LOAD], 16)
                    for j in range(J):
                        dve.bn_stats(stats[:, b * J + j, :], x[:, b, j, :]).then_inc(chain, 1)
                        chain_count[0] += 1

            stats_of(range(NB // 2))
            dve.wait_ge(w_loaded, 16 * N_WDMA)
            dve.tensor_reduce(tern[:, 0:1], w_raw[:, TW, :], AX_X, ALU.add,
                              apply_absolute_value=True).then_inc(tern_sum, 1)
            dve.tensor_scalar(mu[:, 2:4], mu[:, 0:2], -1.0, 1.0, ALU.mult, ALU.add).then_inc(chain, 1)
            chain_count[0] += 1
            dve.wait_ge(wT_ready, 1)
            for half in range(2):
                dve.tensor_copy(wT[:, 4 * half:4 * half + 4, :],
                                banks[half][:, :].rearrange("p (k c) -> p k c", k=4)).then_inc(chain, 1)
                chain_count[0] += 1
            dve.wait_ge(chain, chain_count[0])
            dve.tensor_scalar(wr_now[:, :], wT[:, FR, :], mu[:, 0:1], None, ALU.mult).then_inc(w_ready, 1)
            dve.tensor_scalar(wr_prev[:, :], wT[:, FR, :], mu[:, 2:3], None, ALU.mult).then_inc(w_ready, 1)
            dve.tensor_scalar(wT[:, FV, :], wT[:, FV, :], 0.5, None, ALU.mult).then_inc(w_ready, 1)
            dve.wait_ge(tern_sum, 2)
            chained(dve, dve.tensor_scalar(tern[:, 1:2], banks[2][:, 0:1], 1.0 / (C * C), 0.7, ALU.mult, ALU.mult))
            chained(dve, dve.tensor_scalar(tern[:, 2:3], tern[:, 1:2], -1.0, None, ALU.mult))
            chained(dve, dve.tensor_scalar(ternm[:, :], wT[:, TW, :], tern[:, 2:3], None, ALU.is_lt))
            chained(dve, dve.scalar_tensor_tensor(out=wT[:, TW, :], in0=wT[:, TW, :], scalar=tern[:, 1:2],
                                                  in1=ternm[:, :], op0=ALU.is_gt, op1=ALU.subtract))
            dve.tensor_scalar(wT[:, TW, :], wT[:, TW, :], alpha_b[:, 0:1], 0.5, ALU.mult, ALU.mult).then_inc(w_ready, 1)
            stats_of(range(NB // 2, NB))
            dve.wait_ge(bias_loaded, 16 * N_BDMA)
            dve.tensor_scalar(btern_b[:, :, :], btern_b[:, :, :], 0.5, None, ALU.mult).then_inc(w_ready, 1)

        N_WREADY = 5
        ln_done = [0]

        def layer_consts_dve(dve):
            k = ln_done[0]
            ln_done[0] += 1
            me, mo = stats[:, :, 1], stats[:, :, 4]
            m2e, m2o = stats[:, :, 2], stats[:, :, 5]
            a, b, c = lnt[:, 0, :], lnt[:, 1, :], lnt[:, 2, :]
            dve.wait_ge(chain, chain_count[0])
            chained(dve, dve.tensor_tensor(a, me, mo, ALU.subtract))
            chained(dve, dve.tensor_tensor(b, a, a, ALU.mult))
            chained(dve, dve.scalar_tensor_tensor(out=a, in0=b, scalar=0.25 * C, in1=m2e, op0=ALU.mult, op1=ALU.add))
            chained(dve, dve.tensor_tensor(a, a, m2o, ALU.add))
            dve.tensor_scalar(c, a, 1.0 / C, EPS, ALU.mult, ALU.add).then_inc(ln_var, 1)
            dve.wait_ge(ln_var, k + 1)
            chained(dve, dve.tensor_scalar(a, c, -0.5, None, ALU.mult))
            chained(dve, dve.tensor_tensor(b, me, mo, ALU.add))
            dve.wait_ge(ln_std, k + 1)
            chained(dve, dve.reciprocal(c, rstd[:, :]))
            chained(dve, dve.tensor_tensor(nbias[:, :], c, c, ALU.mult))
            chained(dve, dve.tensor_tensor(nbias[:, :], nbias[:, :], a, ALU.mult))
            chained(dve, dve.scalar_tensor_tensor(out=rstd[:, :], in0=nbias[:, :], scalar=1.5, in1=c,
                                                  op0=ALU.add, op1=ALU.mult))
            dve.scalar_tensor_tensor(out=nbias[:, :], in0=b, scalar=-0.5, in1=rstd[:, :],
                                     op0=ALU.mult, op1=ALU.mult).then_inc(ln_ready, 1)
            dve.wait_ge(ln_ready, k + 1)

        def layer_consts_act(act, k):
            act.wait_ge(consts_ready, 4)
            act.activation(warm[:, k:k + 1], ones[:, k:k + 1], ACT.Sqrt)
            act.wait_ge(ln_var, k + 1)
            act.activation(rstd[:, :], lnt[:, 2, :], ACT.Sqrt).then_inc(ln_std, 1)

        def normalise(eng, out, n, chunks=range(J)):
            for j in chunks:
                at = n * J + j
                ins = eng.tensor_scalar(out[:, j, :], x_chunks[:, bass.ds(at, 1), :].rearrange("p o c -> p (o c)"),
                                        rstd[:, bass.ds(at, 1)], nbias[:, bass.ds(at, 1)], ALU.mult, ALU.add)
            return ins

        def add_stats(dve, n, sems):
            for j in range(J):
                at = n * J + j
                dve.bn_stats(stats[:, bass.ds(at, 1), :].rearrange("p o s -> p (o s)"),
                             x_chunks[:, bass.ds(at, 1), :].rearrange("p o c -> p (o c)")).then_inc(sems, 1)

        def seq(n):
            return x[:, bass.ds(n, 1), :, :].rearrange("p o j c -> p (o j) c")

        def ffn_layer(layer):
            names = ("xn_ready t_ready xT_ready xk_now_ready xk_prev_ready xk_ready k_ready r_ready relu_ready "
                     "gate_ready kact_ready kv_ready gated updated stats").split()
            q = {n: sem(f"f{layer}_{n}") for n in names}
            LAG = 8
            T_BANK, K_BANK, R_BANK, KV_BANK = (0, 1), (2, 3), (4, 5), (6, 7)
            PROJECT, VALUE, GATE, UPDATE = 1, 3, 3, 4

            def pool(eng):
                def step(t):
                    if t.within(NB):
                        s = t.parity
                        eng.wait_ge(q["xk_prev_ready"], t.n + 1)
                        eng.wait_ge(q["xk_now_ready"], t.n + 1)
                        eng.tensor_tensor(xk[:, s, :], xk[:, s, :], xk_prev[:, s, 0:S], ALU.add).then_inc(q["xk_ready"], 1)
                    k = t.back(PROJECT)
                    if k.within(NB):
                        s = k.parity
                        eng.wait_ge(q["relu_ready"], k.n + 1)
                        wait(eng, q["kv_ready"], k.n - 1)
                        eng.tensor_tensor(kact[:, s, :], relu[:, s, :], relu[:, s, :],
                                          ALU.mult).then_inc(q["kact_ready"], 1)
                run_steps(eng, NB, LAG, step)

            def pe(eng):
                if layer == 0:
                    eng.wait_ge(w_ready, N_WREADY)

                def step(t):
                    v = t.back(VALUE)
                    if v.within(NB):
                        s = v.parity
                        eng.wait_ge(q["kact_ready"], v.n + 1)
                        wait(eng, q["gated"], v.n - 1)
                        for j in range(J):
                            mm = eng.matmul(halves(KV_BANK[s])[:, j, :], kact[:, s, j::J], wT[:, FV, :],
                                            start=True, stop=True)
                        mm.then_inc(q["kv_ready"], 1)
                    if t.within(NB):
                        eng.wait_ge(q["xn_ready"], t.n + 1)
                        wait(eng, q["xT_ready"], t.n - 1)
                        for j in range(J):
                            mm = eng.transpose(halves(T_BANK[t.parity])[:, j, :], xn[:, t.parity, j, :], ident[:, :])
                        mm.then_inc(q["t_ready"], 1)
                    k = t.back(PROJECT)
                    if k.within(NB):
                        s = k.parity
                        eng.wait_ge(q["xk_ready"], k.n + 1)
                        wait(eng, q["relu_ready"], k.n - 1)
                        eng.matmul(banks[K_BANK[s]][:, 0:S], wT[:, FK, :], xk[:, s, :], start=True,
                                   stop=True).then_inc(q["k_ready"], 1)
                        eng.wait_ge(q["xT_ready"], k.n + 1)
                        wait(eng, q["gate_ready"], k.n - 1)
                        for j in range(J):
                            eng.matmul(halves(R_BANK[s])[:, j, :], xT[:, s, 1 + j::J], wr_now[:, :],
                                       start=True, stop=False)
                            mm = eng.matmul(halves(R_BANK[s])[:, j, :], xT[:, s, j:S:J], wr_prev[:, :],
                                            start=False, stop=True)
                        mm.then_inc(q["r_ready"], 1)
                run_steps(eng, NB, LAG, step)

            def act(eng):
                layer_consts_act(eng, layer)

                def step(t):
                    if t.within(NB):
                        s = t.parity

                        def tokens(tile):
                            return tile.rearrange("c (p j) -> c j p", j=J)
                        eng.wait_ge(q["t_ready"], t.n + 1)
                        wait(eng, q["xk_ready"], t.n - 1)
                        eng.activation(tokens(xk_prev[:, s, 1:1 + S]), halves(T_BANK[s]), ACT.Copy,
                                       scale=mu[:, 3:4]).then_inc(q["xk_prev_ready"], 1)
                        wait(eng, q["k_ready"], t.n - 1)
                        eng.activation(tokens(xk[:, s, :]), halves(T_BANK[s]), ACT.Copy,
                                       scale=mu[:, 1:2]).then_inc(q["xk_now_ready"], 1)
                        wait(eng, q["r_ready"], t.n - 1)
                        eng.copy(tokens(xT[:, s, 1:1 + S]), halves(T_BANK[s])).then_inc(q["xT_ready"], 1)
                    k = t.back(PROJECT)
                    if k.within(NB):
                        s = k.parity
                        eng.wait_ge(q["k_ready"], k.n + 1)
                        wait(eng, q["kact_ready"], k.n - 1)
                        eng.activation(relu[:, s, :], banks[K_BANK[s]][:, 0:S], ACT.Relu).then_inc(q["relu_ready"], 1)
                        eng.wait_ge(q["r_ready"], k.n + 1)
                        wait(eng, q["gated"], k.n - 1)
                        eng.activation(gate[:, s, :, :], halves(R_BANK[s]), ACT.Sigmoid).then_inc(q["gate_ready"], 1)
                run_steps(eng, NB, LAG, step)

            def dve(eng):
                def step(t):
                    if t.within(NB):
                        wait(eng, q["t_ready"], t.n - 1)
                        normalise(eng, xn[:, t.parity], t.n).then_inc(q["xn_ready"], 1)
                    u = t.back(UPDATE)
                    if u.within(NB):
                        eng.wait_ge(q["gated"], u.n + 1)
                        eng.tensor_tensor(seq(u.n), seq(u.n), branch[:, u.parity, :, :],
                                          ALU.add).then_inc(q["updated"], 1)
                    if u.within(NB):
                        eng.wait_ge(q["updated"], u.n + 1)
                        add_stats(eng, u.n, q["stats"])
                    g = t.back(GATE)
                    if g.within(NB):
                        s = g.parity
                        eng.wait_ge(q["kv_ready"], g.n + 1)
                        eng.wait_ge(q["gate_ready"], g.n + 1)
                        eng.tensor_tensor(branch[:, s, :, :], halves(KV_BANK[s]), gate[:, s, :, :],
                                          ALU.mult).then_inc(q["gated"], 1)
                run_steps(eng, NB, LAG, step)
                eng.wait_ge(q["stats"], J * NB)

            return pool, pe, act, dve

        work = sb("work", [P, 8 * 2 * S])

        def tile(at, shape):
            n = int(np.prod(shape))
            v = work[:, at * 2 * S:at * 2 * S + n]
            names = "abcd"[:len(shape)]
            sizes = {k: d for k, d in zip(names[1:], shape[1:])}
            return v.rearrange(f"p ({' '.join(names)}) -> p {' '.join(names)}", **sizes)

        relu, gate = tile(0, [2, S]), tile(1, [2, J, C])
        kact, branch = tile(2, [2, S]), tile(3, [2, J, C])
        xk = tile(4, [2, S])

        qk = tile(0, [2, 2, S])
        vrow = tile(2, [2, J, C])
        nmax = sb("nmax", [P, 2, J])
        nmax_s = sb("nmax_s", [P, 2, J])
        den = sb("den", [P, 2, J])
        rden = sb("rden", [P, 2, J])
        prob = tile(3, [2, J, S])
        probT = tile(5, [2, J, S])
        orow = tile(7, [2, J, C])

        def attn0_layer(layer):
            names = ("xn_ready t_ready xT_ready qk_ready qk_copied v_ready v_copied s_ready max_ready bias_ready "
                     "exp_ready den_ready pT_ready pT_copied o_ready o_copied y_ready updated stats xb_ready").split()
            q = {n: sem(f"a{layer}_{n}") for n in names}
            LAG = 8
            T_BANK, QK_BANK, V_BANK, PT_BANK, O_BANK, Y_BANK, S_BANK = 0, 1, 2, 3, 4, 5, (6, 7)
            TO_CHANNELS, QK, VALUES, SOFTMAX, TURN, WEIGH, OUTPUT = 1, 2, 3, 3, 4, 5, 6

            def pool(eng):
                eng.wait_ge(ln_ready, layer + 1)

                def step(t):
                    if t.within(NB):
                        eng.wait_ge(q["xn_ready"], t.n + 1)
                        eng.tensor_tensor(seq(t.n), seq(t.n), bproj_b[:, :, :], ALU.add).then_inc(q["xb_ready"], 1)
                run_steps(eng, NB, LAG, step)

            def pe(eng):
                def step(t):
                    a = t.back(QK)
                    if a.within(NB):
                        s = a.parity
                        eng.wait_ge(q["xT_ready"], a.n + 1)
                        wait(eng, q["qk_copied"], a.n)
                        for i, w in enumerate((WQ, WK)):
                            mm = eng.matmul(halves(QK_BANK, S)[:, i, :], wT[:, w, :], xT[:, s, 1:1 + S],
                                            start=True, stop=True)
                        mm.then_inc(q["qk_ready"], 1)
                    o = t.back(WEIGH)
                    if o.within(NB):
                        s = o.parity
                        eng.wait_ge(q["pT_copied"], o.n + 1)
                        eng.wait_ge(q["v_copied"], o.n + 1)
                        wait(eng, q["o_copied"], o.n)
                        for j in range(J):
                            for c in range(J):
                                mm = eng.matmul(halves(O_BANK)[:, j, :], probT[:, s, c, j * P:(j + 1) * P],
                                                vrow[:, s, c, :], start=(c == 0), stop=(c == J - 1))
                        mm.then_inc(q["o_ready"], 1)
                    v = t.back(VALUES)
                    if v.within(NB):
                        s = v.parity
                        wait(eng, q["v_copied"], v.n)
                        for c in range(J):
                            mm = eng.matmul(halves(V_BANK)[:, c, :], xT[:, s, 1 + c * P:1 + (c + 1) * P], wT[:, WV, :],
                                            start=True, stop=True)
                        mm.then_inc(q["v_ready"], 1)
                    y = t.back(OUTPUT)
                    if y.within(NB):
                        eng.wait_ge(q["o_copied"], y.n + 1)
                        wait(eng, q["updated"], y.n)
                        for j in range(J):
                            mm = eng.matmul(halves(Y_BANK)[:, j, :], orow[:, y.parity, j, :], wT[:, WP, :],
                                            start=True, stop=True)
                        mm.then_inc(q["y_ready"], 1)
                    r = t.back(TURN)
                    if r.within(NB):
                        s = r.parity
                        eng.wait_ge(q["exp_ready"], J * (r.n + 1))
                        wait(eng, q["pT_copied"], r.n)
                        for c in range(J):
                            for j in range(J):
                                mm = eng.transpose(halves(PT_BANK, S)[:, c, j * P:(j + 1) * P],
                                                   prob[:, s, j, c * P:(c + 1) * P], ident[:, :])
                        mm.then_inc(q["pT_ready"], 1)
                    if a.within(NB):
                        s = a.parity
                        eng.wait_ge(q["qk_copied"], a.n + 1)
                        wait(eng, q["exp_ready"], J * (a.n - 1))
                        for j in range(J):
                            mm = eng.matmul(halves(S_BANK[s], S)[:, j, :], qk[:, s, 0, j * P:(j + 1) * P],
                                            qk[:, s, 1, :], start=True, stop=True)
                        mm.then_inc(q["s_ready"], 1)
                    if t.within(NB):
                        eng.wait_ge(q["xn_ready"], t.n + 1)
                        wait(eng, q["xT_ready"], t.n)
                        for j in range(J):
                            mm = eng.transpose(halves(T_BANK)[:, j, :], xn[:, t.parity, j, :], ident[:, :])
                        mm.then_inc(q["t_ready"], 1)
                run_steps(eng, NB, LAG, step)

            def act(eng):
                layer_consts_act(eng, layer)

                def step(t):
                    a = t.back(QK)
                    if a.within(NB):
                        s = a.parity
                        eng.wait_ge(q["qk_ready"], a.n + 1)
                        wait(eng, q["s_ready"], a.n - 1)
                        eng.copy(qk[:, s, :, :], halves(QK_BANK, S)).then_inc(q["qk_copied"], 1)
                    x_ = t.back(TO_CHANNELS)
                    if x_.within(NB):
                        eng.wait_ge(q["t_ready"], x_.n + 1)
                        wait(eng, q["v_ready"], x_.n - 1)
                        eng.copy(xT[:, x_.parity, 1:1 + S].rearrange("c (p j) -> c j p", j=J),
                                 halves(T_BANK)).then_inc(q["xT_ready"], 1)
                    v = t.back(VALUES)
                    if v.within(NB):
                        eng.wait_ge(q["v_ready"], v.n + 1)
                        wait(eng, q["o_ready"], v.n - 1)
                        eng.copy(vrow[:, v.parity, :, :], halves(V_BANK)).then_inc(q["v_copied"], 1)
                    e = t.back(SOFTMAX)
                    if e.within(NB):
                        s = e.parity
                        eng.wait_ge(q["bias_ready"], e.n + 1)
                        wait(eng, q["pT_ready"], e.n - 1)
                        wait(eng, q["den_ready"], e.n - 1)
                        for j in range(J):
                            eng.activation(prob[:, s, j, :], halves(S_BANK[s], S)[:, j, :], ACT.Exp,
                                           bias=nmax_s[:, s, j:j + 1], scale=ATTN0_SCALE,
                                           accum_out=den[:, s, j:j + 1]).then_inc(q["exp_ready"], 1)
                run_steps(eng, NB, LAG, step)

            def dve(eng):
                def step(t):
                    o = t.back(WEIGH)
                    if o.within(NB):
                        s = o.parity
                        eng.wait_ge(q["den_ready"], o.n + 1)
                        eng.wait_ge(q["o_ready"], o.n + 1)
                        wait(eng, q["y_ready"], o.n - 1)
                        eng.tensor_tensor(orow[:, s, :, :], halves(O_BANK),
                                          rden[:, s, :].unsqueeze(2).to_broadcast([P, J, C]),
                                          ALU.mult).then_inc(q["o_copied"], 1)
                    if t.within(NB):
                        wait(eng, q["t_ready"], t.n - 1)
                        normalise(eng, xn[:, t.parity], t.n).then_inc(q["xn_ready"], 1)
                    r = t.back(TURN)
                    if r.within(NB):
                        eng.wait_ge(q["pT_ready"], r.n + 1)
                        wait(eng, q["o_ready"], r.n - 1)
                        eng.tensor_copy(probT[:, r.parity, :, :], halves(PT_BANK, S)).then_inc(q["pT_copied"], 1)
                    a = t.back(QK)
                    if a.within(NB):
                        eng.wait_ge(q["s_ready"], a.n + 1)
                        eng.tensor_reduce(nmax[:, a.parity, :], halves(S_BANK[a.parity], S), AX_X, ALU.max,
                                          negate=True).then_inc(q["max_ready"], 1)
                    e = t.back(SOFTMAX)
                    if e.within(NB):
                        eng.wait_ge(q["exp_ready"], J * (e.n + 1))
                        wait(eng, q["o_copied"], e.n - 1)
                        eng.reciprocal(rden[:, e.parity, :], den[:, e.parity, :]).then_inc(q["den_ready"], 1)
                    y = t.back(OUTPUT)
                    if y.within(NB):
                        eng.wait_ge(q["y_ready"], y.n + 1)
                        eng.wait_ge(q["xb_ready"], y.n + 1)
                        eng.tensor_tensor(seq(y.n), seq(y.n), halves(Y_BANK), ALU.add).then_inc(q["updated"], 1)
                        eng.wait_ge(q["updated"], y.n + 1)
                        add_stats(eng, y.n, q["stats"])
                    if a.within(NB):
                        eng.wait_ge(q["max_ready"], a.n + 1)
                        wait(eng, q["exp_ready"], J * (a.n - 1))
                        eng.tensor_scalar(nmax_s[:, a.parity, :], nmax[:, a.parity, :], ATTN0_SCALE, None,
                                          ALU.mult).then_inc(q["bias_ready"], 1)
                run_steps(eng, NB, LAG, step)
                eng.wait_ge(q["stats"], J * NB)

            return pool, pe, act, dve

        def tern_layer(layer, last):
            names = "xn_ready xn_odd_ready t_ready xT_ready y_ready updated stats xb_ready".split()
            q = {n: sem(f"t{layer}_{n}") for n in names}
            LAG = 8
            TO_CHANNELS, PROJECT, UPDATE, STATS = 1, 2, 3, 4

            def pool(eng):
                eng.wait_ge(ln_ready, layer + 1)

                def step(t):
                    if t.within(NB):
                        eng.wait_ge(q["xn_ready"], t.n + 1)
                        eng.wait_ge(q["xn_odd_ready"], t.n + 1)
                        eng.tensor_tensor(seq(t.n), seq(t.n), btern_b[:, :, :], ALU.add).then_inc(q["xb_ready"], 1)
                run_steps(eng, NB, LAG, step)

            def pe(eng):
                def step(t):
                    k = t.back(PROJECT)
                    if k.within(NB):
                        s = k.parity
                        eng.wait_ge(q["xT_ready"], k.n + 1)
                        wait(eng, q["updated"], k.n - 1)
                        for j in range(J):
                            mm = eng.matmul(halves(2 + s)[:, j, :], xT[:, s, 1 + j * P:1 + (j + 1) * P], wT[:, TW, :],
                                            start=True, stop=True)
                        mm.then_inc(q["y_ready"], 1)
                    if t.within(NB):
                        eng.wait_ge(q["xn_ready"], t.n + 1)
                        eng.wait_ge(q["xn_odd_ready"], t.n + 1)
                        wait(eng, q["xT_ready"], t.n - 1)
                        for j in range(J):
                            mm = eng.transpose(halves(t.parity)[:, j, :], xn[:, t.parity, j, :], ident[:, :])
                        mm.then_inc(q["t_ready"], 1)
                run_steps(eng, NB, LAG, step)

            def act(eng):
                layer_consts_act(eng, layer)
                eng.wait_ge(ln_ready, layer + 1)

                def step(t):
                    if t.within(NB):
                        at = t.n * J + 1
                        wait(eng, q["t_ready"], t.n - 1)
                        eng.activation(xn[:, t.parity, 1, :], x_chunks[:, bass.ds(at, 1), :].rearrange("p o c -> p (o c)"),
                                       ACT.Identity, bias=nbias[:, bass.ds(at, 1)],
                                       scale=rstd[:, bass.ds(at, 1)]).then_inc(q["xn_odd_ready"], 1)
                    c = t.back(TO_CHANNELS)
                    if c.within(NB):
                        eng.wait_ge(q["t_ready"], c.n + 1)
                        wait(eng, q["y_ready"], c.n - 1)
                        eng.copy(xT[:, c.parity, 1:1 + S], banks[c.parity][:, 0:S]).then_inc(q["xT_ready"], 1)
                run_steps(eng, NB, LAG, step)

            def dve(eng):
                def step(t):
                    if t.within(NB):
                        wait(eng, q["t_ready"], t.n - 1)
                        normalise(eng, xn[:, t.parity], t.n, chunks=(0,)).then_inc(q["xn_ready"], 1)
                    d = t.back(STATS)
                    if not last and d.within(NB):
                        eng.wait_ge(q["updated"], d.n + 1)
                        add_stats(eng, d.n, q["stats"])
                    u = t.back(UPDATE)
                    if u.within(NB):
                        eng.wait_ge(q["y_ready"], u.n + 1)
                        eng.wait_ge(q["xb_ready"], u.n + 1)
                        eng.tensor_tensor(seq(u.n), seq(u.n), halves(2 + u.parity), ALU.add).then_inc(q["updated"], 1)
                run_steps(eng, NB, LAG, step)
                if not last:
                    eng.wait_ge(q["stats"], J * NB)

            def sync(eng):
                if last:
                    for b in range(0, NB, LOAD):
                        eng.wait_ge(q["updated"], b + LOAD)
                        eng.dma_start(xout_v[:, b:b + LOAD, :], x_flat[:, b:b + LOAD, :]).then_inc(stored, 16)
                    eng.wait_ge(stored, 16 * (NB // LOAD))

            return pool, pe, act, dve, sync

        wqk_hi = sb("wqk_hi", [P, 2, H * D], F32R)
        wqk_lo = sb("wqk_lo", [P, 2, H * D], F32R)
        wv_hi = sb("wv_hi", [P, H * D], F32R)
        wv_lo = sb("wv_lo", [P, H * D], F32R)
        wout = sb("wout", [P, PAIRS, C])
        bqk = sb("bqk", [P, 2, PAIRS])
        bv_b = sb("bv_b", [P, H * D])
        pos = sb("pos", [P, S])
        x_hi = sb("x_hi", [P, 2, S], F32R)
        x_lo = sb("x_lo", [P, 2, S], F32R)
        qk_parts = sb("qk_parts", [P, 2, 4, PAIRS, S], F32R)
        q_twice = qk_parts[:, :, 0, :, :]
        q_rest = qk_parts[:, :, 3, :, :]
        k_ones = qk_parts[:, :, 1, :, :]
        k_parts = qk_parts[:, :, 2, :, :]
        k_sum = sb("k_sum", [P, 2, S])
        v1 = sb("v1", [P, J, H, VW])
        nm1 = sb("nm1", [P, 2, 2 * J])
        m_rows = sb("m_rows", [2 * J, 2, P], F32R)
        p1 = sb("p1", [P, 2, 2, J, S])
        rden1 = sb("rden1", [P, 2, 2, J])
        o1 = tile(0, [J, H, D])
        o1T = tile(4, [PAIRS, S])

        w1_raw = v1[:, :, :, :].rearrange("p j h w -> p (j h w)")
        assert J * H * VW == 3 * H * D
        w1_loaded = sem("w1_loaded")
        w1_scaled = sem("w1_scaled")
        w1_hi = sem("w1_hi")
        w1_lo = sem("w1_lo")
        attn1_zeroed = sem("attn1_zeroed")
        bqk_scaled = sem("bqk_scaled")

        def attn1_setup_sync(sp):
            sp.dma_start(w1_raw[:, :], W_qkv1[:, :]).then_inc(w1_loaded, 16)
            sp.dma_start(wout[:, :, :], W_out1.rearrange("(i p) e -> p i e", p=P)).then_inc(w1_loaded, 16)
            sp.dma_start(pos[0:D, :], pos_t).then_inc(w1_loaded, 16)
            sp.dma_start(pos[D:P, :], pos_t).then_inc(w1_loaded, 16)
            for i in range(2):
                for pr in range(PAIRS):
                    at = i * H * D + pr * P
                    sp.dma_start(bqk[:, i, pr:pr + 1],
                                 b_qkv1[at:at + P].rearrange("(c o) -> c o", o=1)).then_inc(w1_loaded, 16)
            sp.dma_start(bv_b[:, :], b_qkv1[2 * H * D:3 * H * D].rearrange("(o c) -> o c", o=1)
                         .to_broadcast([P, H * D])).then_inc(w1_loaded, 16)
        N_W1DMA = 4 + 2 * PAIRS + 1

        def attn1_setup_act(act):
            act.wait_ge(w1_loaded, 16 * N_W1DMA)
            act.activation(bqk[:, 0, :], bqk[:, 0, :], ACT.Copy, scale=0.125).then_inc(bqk_scaled, 1)
            act.activation(w1_raw[:, 0:H * D], w1_raw[:, 0:H * D], ACT.Copy, scale=0.125).then_inc(w1_scaled, 1)
            act.wait_ge(w1_scaled, 1)
            act.copy(wqk_hi[:, :, :].rearrange("p z c -> p (z c)"), w1_raw[:, 0:2 * H * D]).then_inc(w1_hi, 1)
            act.copy(wv_hi[:, :], w1_raw[:, 2 * H * D:]).then_inc(w1_hi, 1)

        def attn1_setup_pool(pool):
            for tile in (q_rest, k_ones):
                for par in range(2):
                    pool.memset(tile[:, par].bitcast(F32), 0.0).then_inc(attn1_zeroed, 1)
            pool.wait_ge(attn1_zeroed, 4)
            pool.memset(k_ones[D:D + 1, 0, :, :].bitcast(F32), 1.0).then_inc(attn1_zeroed, 1)
            pool.wait_ge(attn1_zeroed, 5)
            pool.memset(k_ones[0:1, 1, :, :].bitcast(F32), 1.0).then_inc(attn1_zeroed, 1)
            pool.wait_ge(attn1_zeroed, 6)
            pool.wait_ge(w1_hi, 1)
            pool.tensor_tensor(wqk_lo[:, :, :].rearrange("p z c -> p (z c)"), w1_raw[:, 0:2 * H * D],
                               wqk_hi[:, :, :].rearrange("p z c -> p (z c)").bitcast(F32),
                               ALU.subtract).then_inc(w1_lo, 1)
            pool.wait_ge(w1_hi, 2)
            pool.tensor_tensor(wv_lo[:, :], w1_raw[:, 2 * H * D:], wv_hi[:, :].bitcast(F32),
                               ALU.subtract).then_inc(w1_lo, 1)
            pool.wait_ge(w1_lo, 2)
            pool.memset(v1[:, :, :, D:VW], 1.0).then_inc(attn1_zeroed, 1)

        def wait_attn1_ready(eng):
            eng.wait_ge(attn1_zeroed, 7)
            eng.wait_ge(w1_lo, 2)
            eng.wait_ge(bqk_scaled, 1)

        class Pair:

            def __init__(self, b, odd, pr):
                self.b, self.odd, self.pr = b, odd, pr
                self.n = b * PAIRS + pr
                self.slot = pr % 2

            def back(self, lag):
                seqs = (lag - self.pr + PAIRS - 1) // PAIRS if lag > self.pr else 0
                return Pair(self.b - seqs, (self.odd + seqs) % 2, (self.pr - lag) % PAIRS)

            @property
            def exists(self):
                return not isinstance(self.b, int) or 0 <= self.b < NB

        def run_pairs(eng, step):
            for b in (0, 1):
                for pr in range(PAIRS):
                    step(Pair(b, b, pr))
            with eng.Fori(1, NB // 2 - 1) as half:
                for odd in (0, 1):
                    for pr in range(PAIRS):
                        step(Pair(half * 2 + odd, odd, pr))
            for b in (NB - 2, NB - 1, NB):
                for pr in range(PAIRS):
                    step(Pair(b, b % 2, pr))
            step(Pair(NB + 1, 1, 0))

        MISC_USES = [(0, 0, "output", 2, 2), (0, 1, "turn", 0, 1), (1, 1, "values", 0, 0), (2, 0, "turn", 1, 1),
                     (3, 0, "values", 1, 0), (4, 0, "turn", 2, 1), (4, 1, "tokens", 0, -1), (5, 0, "values", 2, 0),
                     (6, 0, "turn", 3, 1), (6, 1, "values", 3, 0), (7, 0, "output", 0, 1), (7, 1, "output", 1, 1)]
        OUT_LAST = 2

        def misc_use(t, place):
            for pr, at, what, part, back in MISC_USES:
                if (pr, at) == (t.pr, place):
                    b = t.b - back
                    if not isinstance(b, int) or 0 <= b < NB:
                        return what, part, b
            return None

        def misc_before(t, place):
            k = [u[:2] for u in MISC_USES].index((t.pr, place))
            b = t.b
            while True:
                k -= 1
                if k < 0:
                    k, b = len(MISC_USES) - 1, b - 1
                if isinstance(b, int) and b < 0:
                    return "tokens", 0, 0
                _, _, what, part, back = MISC_USES[k]
                if not isinstance(b, int) or 0 <= b - back < NB:
                    return what, part, b - back

        def attn1_layer(layer):
            names = ("xn_ready t_ready x_hi_ready x_lo_ready k_ready q_ready q_hi_ready "
                     "q_lo_ready k_sum_ready k_hi_ready k_lo_ready v_ready v_copied max_scored max_ready mT_ready "
                     "mT_copied scores_ready exp_ready pv_ready rden_ready o_copied oT_ready oT_copied "
                     "y_ready updated stats xb_ready").split()
            q = {n: sem(f"b_{n}") for n in names}
            m_placed = [sem(f"b_m_placed{i}") for i in range(2)]
            again_placed = [sem(f"b_again_placed{i}") for i in range(4)]
            Q_BANK, K_BANK, MAX_BANK, MISC, S_BANK, O_BANK = 0, 1, 2, 3, (4, 5), (6, 7)
            HALF = (slice(0, D), slice(D, P))
            VG = J * G
            TG = PAIRS // 2
            SPLIT_Q, MAXIMA, SCORES, WEIGH_ODD = 1, 3, 5, 6

            def o_pair(slot):
                return banks[O_BANK[slot]][:, 0:2 * J * VW].rearrange("p (h j w) -> p h j w", h=2, j=J)

            def pe(eng):
                def scores(u, par):
                    if par == 0:
                        eng.wait_ge(m_placed[u.slot], 32 * (u.b * (PAIRS // 2) + u.pr // 2 + 1))
                        eng.wait_ge(q["q_lo_ready"], 2 * (u.n + 1))
                    wait(eng, q["exp_ready"], 2 * u.n + par - 1)
                    for c in range(J):
                        keys = slice(c * P, (c + 1) * P)
                        out = halves(S_BANK[par], S)[:, c, :]
                        eng.matmul(out, k_parts[:, par, u.pr, keys], q_twice[:, par, u.pr, :], start=True, stop=False)
                        mm = eng.matmul(out, k_ones[:, par, u.pr, keys], q_rest[:, par, u.pr, :],
                                        start=False, stop=True)
                    mm.then_inc(q["scores_ready"], 1)

                def project(u, z):
                    if z == 1 and u.pr == 0:
                        eng.wait_ge(q["x_lo_ready"], u.b + 1)
                    wait(eng, q["k_sum_ready"] if z else q["q_lo_ready"], u.n if z else 2 * u.n)
                    cols = slice(u.pr * P, (u.pr + 1) * P)
                    out = banks[K_BANK if z else Q_BANK][:, 0:S]
                    eng.matmul(out, wqk_hi[:, z, cols], x_hi[:, u.odd, :], start=True, stop=False)
                    eng.matmul(out, wqk_hi[:, z, cols], x_lo[:, u.odd, :], start=False, stop=False)
                    eng.matmul(out, wqk_lo[:, z, cols], x_hi[:, u.odd, :], start=False,
                               stop=True).then_inc(q["k_ready"] if z else q["q_ready"], 1)

                def row_max(u, par):
                    if par == 0:
                        eng.wait_ge(again_placed[u.pr % 4], 32 * (2 * u.b + u.pr // 4 + 1))
                        eng.wait_ge(q["k_lo_ready"], 2 * (u.n + 1))
                        wait(eng, q["mT_copied"], u.n)
                    else:
                        eng.wait_ge(q["max_ready"], 2 * u.n + 1)
                    for j in range(J):
                        mm = eng.matmul(halves(MAX_BANK, S)[:, j, :], q_twice[:, par, u.pr, j * P:(j + 1) * P],
                                        k_parts[:, par, u.pr, :], start=True, stop=True)
                    mm.then_inc(q["max_scored"], 1)

                def turn_maxima(u):
                    eng.wait_ge(q["max_ready"], 2 * (u.n + 1))
                    eng.transpose(banks[MAX_BANK][0:2 * J, 0:P], nm1[:, u.slot, :],
                                  ident[:, :]).then_inc(q["mT_ready"], 1)

                def weigh(u, par):
                    eng.wait_ge(q["exp_ready"], 2 * u.n + par + 1)
                    if par == 0:
                        if u.pr % PG == 0:
                            eng.wait_ge(q["v_copied"], u.b * VG + J * (u.pr // PG + 1))
                        wait(eng, q["o_copied"], u.n - 1)
                    for j in range(J):
                        for c in range(J):
                            mm = eng.matmul(o_pair(u.slot)[:, par, j, :], p1[:, u.slot, par, c, j * P:(j + 1) * P],
                                            v1[:, c, 2 * u.pr + par, :], start=(c == 0), stop=(c == J - 1))
                    mm.then_inc(q["pv_ready"], 1)

                def misc(t, place):
                    use = misc_use(t, place)
                    if use is None:
                        return
                    what, part, b = use
                    last, last_part, last_b = misc_before(t, place)
                    if last == "values":
                        eng.wait_ge(q["v_copied"], last_b * VG + last_part + 1)
                    elif last == "turn":
                        eng.wait_ge(q["oT_copied"], last_b * TG + last_part + 1)
                    elif last == "tokens":
                        eng.wait_ge(q["x_lo_ready"], last_b + 1)
                    elif last_part == OUT_LAST:
                        eng.wait_ge(q["updated"], last_b + 1)
                    if what == "values":
                        g, j = part // J, part % J
                        cols = slice(g * HG * D, (g + 1) * HG * D)
                        toks = slice(j * P, (j + 1) * P)
                        out = banks[MISC][:, :]
                        hi, lo = x_hi[:, t.odd, toks], x_lo[:, t.odd, toks]
                        eng.matmul(out, hi, wv_hi[:, cols], start=True, stop=False)
                        eng.matmul(out, hi, wv_lo[:, cols], start=False, stop=False)
                        eng.matmul(out, lo, wv_hi[:, cols], start=False, stop=True).then_inc(q["v_ready"], 1)
                    elif what == "turn":
                        eng.wait_ge(q["o_copied"], b * PAIRS + 2 * (part + 1))
                        for i in range(2):
                            for j in range(J):
                                mm = eng.transpose(banks[MISC][:, (i * J + j) * P:(i * J + j + 1) * P],
                                                   o1[:, j, 4 * part + 2 * i:4 * part + 2 * i + 2, :]
                                                   .rearrange("p h d -> p (h d)"), ident[:, :])
                        mm.then_inc(q["oT_ready"], 1)
                    elif what == "output":
                        if part == 0:
                            eng.wait_ge(q["oT_copied"], TG * (b + 1))
                        j, pairs = ((0, (0, 1, 2, 3)), (0, (4, 5, 6, 7)), (1, range(PAIRS)))[part]
                        for i in pairs:
                            mm = eng.matmul(halves(MISC)[:, j, :], o1T[:, i, j * P:(j + 1) * P],
                                            wout[:, i, :], start=(i == 0), stop=(i == PAIRS - 1))
                        if part == OUT_LAST:
                            mm.then_inc(q["y_ready"], 1)
                    else:
                        turn_tokens(b)

                def turn_tokens(b):
                    eng.wait_ge(q["xn_ready"], b + 1)
                    for j in range(J):
                        mm = eng.transpose(halves(MISC)[:, j, :], xn[:, 0, j, :], ident[:, :])
                    mm.then_inc(q["t_ready"], 1)

                def step(t):
                    m, b, w = t.back(MAXIMA), t.back(SCORES), t.back(WEIGH_ODD)
                    if m.exists:
                        row_max(m, 0)
                    if t.exists:
                        project(t, 1)
                    if w.exists:
                        weigh(w, 1)
                    if m.exists:
                        row_max(m, 1)
                    misc(t, 0)
                    if b.exists:
                        scores(b, 0)
                        scores(b, 1)
                    if m.exists:
                        turn_maxima(m)
                    if t.exists:
                        project(t, 0)
                    misc(t, 1)
                    if b.exists:
                        weigh(b, 0)

                wait_attn1_ready(eng)
                turn_tokens(0)
                run_pairs(eng, step)

            def act(eng):
                layer_consts_act(eng, layer)
                wait_attn1_ready(eng)

                def exp(u, par):
                    eng.wait_ge(q["scores_ready"], 2 * u.n + par + 1)
                    wait(eng, q["pv_ready"], 2 * (u.n - 2) + par + 1)
                    eng.activation(p1[:, u.slot, par, :, :], halves(S_BANK[par], S), ACT.Exp).then_inc(q["exp_ready"], 1)

                def token_hi(b, odd):
                    eng.wait_ge(q["t_ready"], b + 1)
                    eng.copy(x_hi[:, odd, :], banks[MISC][:, 0:S]).then_inc(q["x_hi_ready"], 1)

                def misc(t, place):
                    use = misc_use(t, place)
                    if use is None:
                        return
                    what, part, b = use
                    if what == "turn":
                        eng.wait_ge(q["oT_ready"], b * TG + part + 1)
                        wait(eng, q["y_ready"], b)
                        eng.copy(o1T[:, 2 * part:2 * part + 2, :], halves(MISC, S)).then_inc(q["oT_copied"], 1)
                    elif what == "tokens":
                        token_hi(b, 1 - t.odd)

                def step(t):
                    b = t.back(SCORES)
                    misc(t, 0)
                    if b.exists:
                        exp(b, 0)
                        exp(b, 1)
                    misc(t, 1)
                    if t.exists:
                        eng.wait_ge(q["k_sum_ready"], t.n + 1)
                        for par in range(2):
                            r = HALF[par]
                            eng.copy(k_ones[r, par, t.pr, :], k_sum[r, t.slot, :]).then_inc(q["k_hi_ready"], 1)
                        eng.wait_ge(q["q_ready"], t.n + 1)
                        for par in range(2):
                            r = HALF[par]
                            eng.activation(q_twice[r, par, t.pr, :], banks[Q_BANK][r, 0:S], ACT.Identity,
                                           bias=bqk[r, 0, t.pr:t.pr + 1]).then_inc(q["q_hi_ready"], 1)

                token_hi(0, 0)
                run_pairs(eng, step)

            def dve(eng):
                wait_attn1_ready(eng)

                def norm(u):
                    eng.wait_ge(q["pv_ready"], 2 * (u.n + 1))
                    wait(eng, q["o_copied"], u.n - 1)
                    eng.reciprocal(rden1[:, u.slot, :, :], o_pair(u.slot)[:, :, :, D]).then_inc(q["rden_ready"], 1)
                    eng.wait_ge(q["rden_ready"], u.n + 1)
                    wait(eng, q["oT_ready"], (u.b - 1) * TG + u.pr // 2 + 1)
                    eng.tensor_tensor(o1[:, :, 2 * u.pr:2 * u.pr + 2, :].rearrange("p j h d -> p h j d"),
                                      o_pair(u.slot)[:, :, :, 0:D],
                                      rden1[:, u.slot, :, :].unsqueeze(3).to_broadcast([P, 2, J, D]),
                                      ALU.mult).then_inc(q["o_copied"], 1)

                def reduce(u, par):
                    eng.wait_ge(q["max_scored"], 2 * u.n + par + 1)
                    wait(eng, q["mT_ready"], u.n - 1)
                    eng.tensor_reduce(nm1[:, u.slot, par * J:(par + 1) * J], halves(MAX_BANK, S), AX_X, ALU.max,
                                      negate=True).then_inc(q["max_ready"], 1)

                def token_lo(b, odd):
                    eng.wait_ge(q["x_hi_ready"], b + 1)
                    eng.tensor_tensor(x_lo[:, odd, :], banks[MISC][:, 0:S], x_hi[:, odd, :].bitcast(F32),
                                      ALU.subtract).then_inc(q["x_lo_ready"], 1)

                def misc(t, place):
                    use = misc_use(t, place)
                    if use is None:
                        return
                    what, part, b = use
                    if what == "values":
                        g, j = part // J, part % J
                        cols = slice(g * HG * D, (g + 1) * HG * D)
                        eng.wait_ge(q["v_ready"], b * VG + part + 1)
                        wait(eng, q["pv_ready"], (b - 1) * H + (g + 1) * HG)
                        eng.tensor_tensor(v1[:, j, g * HG:(g + 1) * HG, 0:D],
                                          banks[MISC][:, :].rearrange("p (h d) -> p h d", d=D),
                                          bv_b[:, cols].rearrange("p (h d) -> p h d", d=D),
                                          ALU.add).then_inc(q["v_copied"], 1)
                    elif what == "output" and part == OUT_LAST:
                        eng.wait_ge(q["y_ready"], b + 1)
                        eng.wait_ge(q["xb_ready"], b + 1)
                        eng.tensor_tensor(seq(b), seq(b), halves(MISC), ALU.add).then_inc(q["updated"], 1)
                        eng.wait_ge(q["updated"], b + 1)
                        add_stats(eng, b, q["stats"])
                    elif what == "tokens":
                        token_lo(b, 1 - t.odd)

                def step(t):
                    h, m, w = t.back(SPLIT_Q), t.back(MAXIMA), t.back(WEIGH_ODD)
                    if t.pr == 3 and (not isinstance(t.b, int) or t.b < NB - 1):
                        eng.wait_ge(q["t_ready"], t.b + 1)
                        normalise(eng, xn[:, 0], t.b + 1).then_inc(q["xn_ready"], 1)
                    if m.exists:
                        reduce(m, 0)
                    if h.exists:
                        for par in range(2):
                            r = HALF[par]
                            eng.wait_ge(q["q_hi_ready"], 2 * h.n + par + 1)
                            eng.scalar_tensor_tensor(out=q_rest[r, par, h.pr, :], in0=banks[Q_BANK][r, 0:S],
                                                     scalar=bqk[r, 0, h.pr:h.pr + 1],
                                                     in1=q_twice[r, par, h.pr, :].bitcast(F32),
                                                     op0=ALU.add, op1=ALU.subtract).then_inc(q["q_lo_ready"], 1)
                    if m.exists:
                        reduce(m, 1)
                    misc(t, 0)
                    if m.exists:
                        eng.wait_ge(q["mT_ready"], m.n + 1)
                        wait(eng, m_placed[m.slot], 32 * (m.b * (PAIRS // 2) + m.pr // 2))
                        eng.tensor_copy(m_rows[:, m.slot, :], banks[MAX_BANK][0:2 * J, 0:P]).then_inc(q["mT_copied"], 1)
                    if t.exists:
                        eng.wait_ge(q["k_ready"], t.n + 1)
                        wait(eng, q["k_lo_ready"], 2 * (t.n - 1))
                        wait(eng, q["k_hi_ready"], 2 * (t.n - 1))
                        eng.scalar_tensor_tensor(out=k_sum[:, t.slot, :], in0=banks[K_BANK][:, 0:S],
                                                 scalar=bqk[:, 1, t.pr:t.pr + 1], in1=pos[:, :], op0=ALU.add,
                                                 op1=ALU.add).then_inc(q["k_sum_ready"], 1)
                    if w.exists:
                        norm(w)
                    misc(t, 1)

                normalise(eng, xn[:, 0], 0).then_inc(q["xn_ready"], 1)
                token_lo(0, 0)
                run_pairs(eng, step)
                eng.wait_ge(q["stats"], J * NB)

            def pool(eng):
                eng.wait_ge(ln_ready, layer + 1)

                def step(t):
                    if not t.exists:
                        return
                    for par in range(2):
                        r = HALF[par]
                        eng.wait_ge(q["k_hi_ready"], 2 * t.n + par + 1)
                        wait(eng, q["k_lo_ready"], 2 * t.n + par)
                        eng.tensor_tensor(k_parts[r, par, t.pr, :], k_sum[r, t.slot, :],
                                          k_ones[r, par, t.pr, :].bitcast(F32), ALU.subtract).then_inc(q["k_lo_ready"], 1)
                    if t.pr == 2:
                        eng.wait_ge(q["k_lo_ready"], 2 * (t.n + 1))
                        eng.wait_ge(q["xn_ready"], t.b + 1)
                        eng.tensor_tensor(seq(t.b), seq(t.b), bout_b[:, :, :], ALU.add).then_inc(q["xb_ready"], 1)
                run_pairs(eng, step)

            def sync(eng):
                def step(t):
                    h, m = t.back(SPLIT_Q), t.back(MAXIMA)
                    if h.exists:
                        for par in range(2):
                            r, o = HALF[par], HALF[1 - par]
                            eng.wait_ge(q["q_hi_ready"], 2 * h.n + par + 1)
                            eng.wait_ge(q["k_hi_ready"], 2 * h.n + par + 1)
                            eng.dma_start(qk_parts[o, par, 0:3:2, h.pr, :].bitcast(F32),
                                          qk_parts[r, par, 0:2, h.pr, :].bitcast(F32)
                                          ).then_inc(again_placed[h.pr % 4], 16)
                    if m.exists:
                        eng.wait_ge(q["mT_copied"], m.n + 1)
                        for par, row in ((0, D), (1, 0)):
                            eng.dma_start(q_rest[row:row + 1, par, m.pr, :].bitcast(F32)
                                          .rearrange("o (j p) -> o j p", j=J),
                                          m_rows[par * J:(par + 1) * J, m.slot, :].bitcast(F32)
                                          ).then_inc(m_placed[m.slot], 16)
                run_pairs(eng, step)

            return pool, pe, act, dve, sync

        ffn_a = ffn_layer(0)
        attn_b = attn0_layer(1)
        ffn_c = ffn_layer(2)
        tern_d = tern_layer(3, last=False)
        attn_e = attn1_layer(4)
        tern_f = tern_layer(5, last=True)
        layers = (ffn_a, attn_b, ffn_c, tern_d, attn_e, tern_f)

        block = ctx.enter_context(nc.Block())

        @block.sync
        def _(sp):
            setup_sync(sp)
            attn1_setup_sync(sp)
            attn_e[4](sp)
            tern_f[4](sp)

        @block.gpsimd
        def _(pool):
            setup_pool(pool)
            for layer in layers:
                if layer is ffn_c:
                    attn1_setup_pool(pool)
                layer[0](pool)

        @block.tensor
        def _(pe):
            setup_pe(pe)
            for layer in layers:
                layer[1](pe)

        @block.scalar
        def _(act):
            for layer in layers:
                if layer is attn_b:
                    attn1_setup_act(act)
                layer[2](act)

        @block.vector
        def _(dve):
            setup_dve(dve)
            for layer in layers:
                layer_consts_dve(dve)
                layer[3](dve)


_INS = ['L0_attn_x', 'L0_attn_w_qkv', 'L0_attn_w_proj', 'L0_attn_b_proj', 'L0_ffn_W_r', 'L0_ffn_W_k', 'L0_ffn_W_v',
        'L0_ffn_mu_r', 'L0_ffn_mu_k', 'L1_attn_W_qkv', 'L1_attn_b_qkv', 'L1_attn_W_out', 'L1_attn_b_out',
        'L1_ffn_weight', 'L1_ffn_alpha', 'L1_ffn_bias']


def position_table():
    positions = np.arange(S, dtype=np.float32)[:, None]
    div = np.exp(np.arange(0, D, 2, dtype=np.float32) * np.float32(-(np.log(10000.0) / D)))
    table = np.zeros((S, D), np.float32)
    table[:, 0::2] = np.sin(positions * div)
    table[:, 1::2] = np.cos(positions * div)
    return np.ascontiguousarray(table.reshape(P, J, D).transpose(2, 1, 0).reshape(D, S))


def kernel(**inputs):
    import concourse.bacc as _bacc
    from concourse.bass_utils import run_bass_kernel_spmd as _run

    nc = _bacc.Bacc("TRN2", target_bir_lowering=False, num_devices=1)
    arrays, args = {}, []
    for name in _INS:
        a = np.ascontiguousarray(inputs[name])
        arrays[f"in_{name}"] = a
        args.append(nc.dram_tensor(f"in_{name}", a.shape, mybir.dt.from_np(a.dtype), kind="ExternalInput").ap())
    arrays["position_table"] = position_table()
    args.append(nc.dram_tensor("position_table", (D, S), F32, kind="ExternalInput").ap())
    args.append(nc.dram_tensor("out", (NB, S, C), F32, kind="ExternalOutput").ap())
    macaron_kernel(nc, *args)
    r = _run(nc, [arrays], core_ids=[0])
    return r.results[0]["out"]
```
